# Optimizing a Trainium2 kernel written in Bass

```python
import numpy as np
import jax
import jax.numpy as jnp

def _softmax(x, axis=-1):
    return jax.nn.softmax(x, axis=axis)

def _gelu(x):
    return jax.nn.gelu(x, approximate=True)

def _silu(x):
    return jax.nn.silu(x)

def _sigmoid(x):
    return jax.nn.sigmoid(x)

def _layernorm(x, axis=-1, eps=1e-05):
    m = jnp.mean(x, axis=axis, keepdims=True)
    v = jnp.var(x, axis=axis, keepdims=True)
    return (x - m) / jnp.sqrt(v + eps)

def _scatter_add(tgt, idx, src, axis=0):
    return tgt.at[idx].add(src)

def _segment_sum(src, seg, n):
    return jax.ops.segment_sum(src, seg, n)
kernel_name = 'mk_hybrid_d1_jaxref_r4_895a68'

def setup_inputs(seed: int=0):
    np.random.seed(seed)
    _w = jnp.asarray

    def _L0_attn_a_setup():
        import jax, jax.numpy as jnp
        import numpy as np
        B, S, D, H = (4, 1024, 256, 16)
        HD = D // H
        EPS = 1e-06

        def _feature_map(t):
            return jax.nn.elu(t) + 1.0
        key = jax.random.key(seed)
        ks = jax.random.split(key, 5)
        scale = 0.02
        return {'x': jax.random.normal(ks[0], (B, S, D), dtype=jnp.float32), 'wq': jax.random.normal(ks[1], (D, D), dtype=jnp.float32) * scale, 'wk': jax.random.normal(ks[2], (D, D), dtype=jnp.float32) * scale, 'wv': jax.random.normal(ks[3], (D, D), dtype=jnp.float32) * scale, 'wo': jax.random.normal(ks[4], (D, D), dtype=jnp.float32) * scale}
    _L0_attn_a_in = _L0_attn_a_setup()

    def _L0_attn_b_setup():
        import jax, jax.numpy as jnp
        import numpy as np
        import math
        N_EMBD = 256
        N_HEAD = 16
        BLOCK_SIZE = 256
        B, T = (4, 256)
        key = jax.random.key(seed)
        ks = jax.random.split(key, 7)
        C = N_EMBD
        return {'x': jax.random.normal(ks[0], (B, T, C), dtype=jnp.float32), 'Wqk': jax.random.normal(ks[1], (C, 2 * C), dtype=jnp.float32) * 0.02, 'bqk': jnp.zeros((2 * C,), dtype=jnp.float32), 'Wgate': jax.random.normal(ks[2], (C, N_HEAD), dtype=jnp.float32) * 0.02, 'bgate': jnp.zeros((N_HEAD,), dtype=jnp.float32), 'Wproj': jax.random.normal(ks[3], (C, C), dtype=jnp.float32) * 0.02, 'bproj': jnp.zeros((C,), dtype=jnp.float32)}
    _L0_attn_b_in = _L0_attn_b_setup()

    def _L0_ffn_setup():
        import math
        import jax, jax.numpy as jnp
        import numpy as np
        D_MODEL = 256
        NUM_EXPERTS = 8
        D_FF_EXPERT = max(64, int(D_MODEL * 4 * 0.25))
        THRESHOLD = 0.9
        CAP_FACTOR = 1.0
        INIT_STD = 0.02

        def _xmoe_route(probs):
            N, E = probs.shape
            order = jnp.argsort(-probs, axis=-1)
            p_sorted = jnp.take_along_axis(probs, order, axis=-1)
            csum = jnp.cumsum(p_sorted, axis=-1)
            reached = (csum >= THRESHOLD).at[:, -1].set(True)
            k_idx = jnp.argmax(reached, axis=-1)
            select_prefix = jnp.arange(E)[None, :] <= k_idx[:, None]
            rows = jnp.arange(N)[:, None]
            assign_mask = jnp.zeros((N, E), dtype=bool).at[rows, order].set(select_prefix)
            rank = jnp.arange(1, E + 1, dtype=probs.dtype)[None, :]
            R_sorted = jnp.where(select_prefix, p_sorted - rank, jnp.full_like(p_sorted, -1000000000.0))
            R = jnp.zeros((N, E), dtype=probs.dtype).at[rows, order].set(R_sorted)
            capacity = int(math.ceil(N / E) * CAP_FACTOR)
            C = min(capacity, N)
            tok_order = jnp.argsort(-R, axis=0)
            topC = tok_order[:C, :]
            keep = jnp.zeros((N, E), dtype=bool).at[topC, jnp.arange(E)[None, :]].set(True)
            final_mask = assign_mask & keep
            return jnp.where(final_mask, probs, jnp.zeros_like(probs))
        key = jax.random.key(seed)
        k_x, k_g, k_w1, k_w2 = jax.random.split(key, 4)
        B, T = (4, 512)
        x = jax.random.normal(k_x, (B, T, D_MODEL), dtype=jnp.float32)
        bound = 1.0 / math.sqrt(D_MODEL)
        gate_w = jax.random.uniform(k_g, (NUM_EXPERTS, D_MODEL), minval=-bound, maxval=bound, dtype=jnp.float32)
        w1 = INIT_STD * jax.random.normal(k_w1, (NUM_EXPERTS, D_FF_EXPERT, D_MODEL), dtype=jnp.float32)
        w2 = INIT_STD * jax.random.normal(k_w2, (NUM_EXPERTS, D_MODEL, D_FF_EXPERT), dtype=jnp.float32)
        return {'x': x, 'gate_w': gate_w, 'w1': w1, 'w2': w2}
    _L0_ffn_in = _L0_ffn_setup()
    _d = {'L0_attn_a_x': _L0_attn_a_in['x'], 'L0_attn_a_wq': _L0_attn_a_in['wq'], 'L0_attn_a_wk': _L0_attn_a_in['wk'], 'L0_attn_a_wv': _L0_attn_a_in['wv'], 'L0_attn_a_wo': _L0_attn_a_in['wo'], 'L0_attn_b_Wqk': _L0_attn_b_in['Wqk'], 'L0_attn_b_bqk': _L0_attn_b_in['bqk'], 'L0_attn_b_Wgate': _L0_attn_b_in['Wgate'], 'L0_attn_b_bgate': _L0_attn_b_in['bgate'], 'L0_attn_b_Wproj': _L0_attn_b_in['Wproj'], 'L0_attn_b_bproj': _L0_attn_b_in['bproj'], 'L0_ffn_gate_w': _L0_ffn_in['gate_w'], 'L0_ffn_w1': _L0_ffn_in['w1'], 'L0_ffn_w2': _L0_ffn_in['w2']}
    _x0 = _d['L0_attn_a_x']
    _d['L0_attn_a_x'] = jax.random.normal(jax.random.fold_in(jax.random.key(seed), 1), (2, 2048, 256), dtype=_x0.dtype)
    del _x0
    return _d

def reference(L0_attn_a_x, L0_attn_a_wq, L0_attn_a_wk, L0_attn_a_wv, L0_attn_a_wo, L0_attn_b_Wqk, L0_attn_b_bqk, L0_attn_b_Wgate, L0_attn_b_bgate, L0_attn_b_Wproj, L0_attn_b_bproj, L0_ffn_gate_w, L0_ffn_w1, L0_ffn_w2):

    def _L0_attn_a_ref(x, wq, wk, wv, wo):
        import jax, jax.numpy as jnp
        import numpy as np
        B, S, D, H = (4, 1024, 256, 16)
        HD = D // H
        EPS = 1e-06

        def _feature_map(t):
            return jax.nn.elu(t) + 1.0
        b, s, d = x.shape
        q = _feature_map((x @ wq).reshape(b, s, H, HD))
        k = _feature_map((x @ wk).reshape(b, s, H, HD))
        v = (x @ wv).reshape(b, s, H, HD)
        qs = jnp.moveaxis(q, 1, 0)
        ks = jnp.moveaxis(k, 1, 0)
        vs = jnp.moveaxis(v, 1, 0)

        def step(carry, qkv):
            S_kv, z = carry
            qt, kt, vt = qkv
            S_kv = S_kv + jnp.einsum('bhd,bhe->bhde', kt, vt)
            z = z + kt
            num = jnp.einsum('bhd,bhde->bhe', qt, S_kv)
            den = jnp.einsum('bhd,bhd->bh', qt, z)[..., None] + EPS
            return ((S_kv, z), num / den)
        init = (jnp.zeros((b, H, HD, HD), x.dtype), jnp.zeros((b, H, HD), x.dtype))
        _, outs = jax.lax.scan(step, init, (qs, ks, vs))
        out = jnp.moveaxis(outs, 0, 1).reshape(b, s, d) @ wo
        return out

    def _L0_attn_b_ref(x, Wqk, bqk, Wgate, bgate, Wproj, bproj):
        import jax, jax.numpy as jnp
        import numpy as np
        import math
        N_EMBD = 256
        N_HEAD = 16
        BLOCK_SIZE = 256
        B, T = (4, 256)
        Bx, Tx, C = x.shape
        H = N_HEAD
        D = C // H
        windows = jnp.array([max(4, BLOCK_SIZE // 2 ** h) for h in range(H)], dtype=jnp.int32)
        qk = x @ Wqk + bqk
        q, k = jnp.split(qk, 2, axis=-1)
        v = k
        q = q.reshape(Bx, Tx, H, D).transpose(0, 2, 1, 3)
        k = k.reshape(Bx, Tx, H, D).transpose(0, 2, 1, 3)
        v = v.reshape(Bx, Tx, H, D).transpose(0, 2, 1, 3)
        i = jnp.arange(Tx)[:, None]
        j = jnp.arange(Tx)[None, :]
        mask = (j <= i)[None] & (j > i - windows[:, None, None])
        att = jnp.einsum('bhtd,bhsd->bhts', q, k) * (1.0 / math.sqrt(D))
        att = jnp.where(mask[None], att, -jnp.inf)
        att = jax.nn.softmax(att, axis=-1)
        out = jnp.einsum('bhts,bhsd->bhtd', att, v)
        combined = out.transpose(0, 2, 1, 3)
        gates = jax.nn.softmax(x @ Wgate + bgate, axis=-1)
        gated = (combined * gates[..., None]).reshape(Bx, Tx, C)
        return gated @ Wproj + bproj

    def _L0_ffn_ref(x, gate_w, w1, w2):
        import math
        import jax, jax.numpy as jnp
        import numpy as np
        D_MODEL = 256
        NUM_EXPERTS = 8
        D_FF_EXPERT = max(64, int(D_MODEL * 4 * 0.25))
        THRESHOLD = 0.9
        CAP_FACTOR = 1.0
        INIT_STD = 0.02

        def _xmoe_route(probs):
            N, E = probs.shape
            order = jnp.argsort(-probs, axis=-1)
            p_sorted = jnp.take_along_axis(probs, order, axis=-1)
            csum = jnp.cumsum(p_sorted, axis=-1)
            reached = (csum >= THRESHOLD).at[:, -1].set(True)
            k_idx = jnp.argmax(reached, axis=-1)
            select_prefix = jnp.arange(E)[None, :] <= k_idx[:, None]
            rows = jnp.arange(N)[:, None]
            assign_mask = jnp.zeros((N, E), dtype=bool).at[rows, order].set(select_prefix)
            rank = jnp.arange(1, E + 1, dtype=probs.dtype)[None, :]
            R_sorted = jnp.where(select_prefix, p_sorted - rank, jnp.full_like(p_sorted, -1000000000.0))
            R = jnp.zeros((N, E), dtype=probs.dtype).at[rows, order].set(R_sorted)
            capacity = int(math.ceil(N / E) * CAP_FACTOR)
            C = min(capacity, N)
            tok_order = jnp.argsort(-R, axis=0)
            topC = tok_order[:C, :]
            keep = jnp.zeros((N, E), dtype=bool).at[topC, jnp.arange(E)[None, :]].set(True)
            final_mask = assign_mask & keep
            return jnp.where(final_mask, probs, jnp.zeros_like(probs))
        B, T, D = x.shape
        N = B * T
        xf = x.reshape(N, D)
        probs = jax.nn.softmax(xf @ gate_w.T, axis=-1)
        scores_sel = _xmoe_route(probs)
        h = jax.nn.gelu(jnp.einsum('nd,efd->enf', xf, w1), approximate=False)
        y_e = jnp.einsum('enf,edf->end', h, w2)
        y = jnp.einsum('ne,end->nd', scores_sel, y_e)
        return y.reshape(B, T, D)
    x = L0_attn_a_x
    x = x + _L0_attn_a_ref(_layernorm(x, axis=-1), L0_attn_a_wq, L0_attn_a_wk, L0_attn_a_wv, L0_attn_a_wo)
    x = x + _L0_ffn_ref(_layernorm(x, axis=-1), L0_ffn_gate_w, L0_ffn_w1, L0_ffn_w2)
    x = x + _L0_attn_b_ref(_layernorm(x, axis=-1), L0_attn_b_Wqk, L0_attn_b_bqk, L0_attn_b_Wgate, L0_attn_b_bgate, L0_attn_b_Wproj, L0_attn_b_bproj)
    x = x + _L0_ffn_ref(_layernorm(x, axis=-1), L0_ffn_gate_w, L0_ffn_w1, L0_ffn_w2)
    return x

_drawn_inputs = setup_inputs


def setup_inputs(seed=0):
    import zlib

    import numpy as np

    out = dict(_drawn_inputs(seed))
    spreads = {'L0_attn_b_bqk': (0.0, 0.8), 'L0_attn_b_bgate': (0.0, 0.8), 'L0_attn_b_bproj': (0.0, 0.1)}
    factors = {'L0_attn_a_wq': 8.0,
     'L0_attn_a_wk': 8.0,
     'L0_attn_a_wv': 8.0,
     'L0_attn_a_wo': 8.0,
     'L0_attn_b_Wqk': 8.0,
     'L0_attn_b_Wgate': 8.0,
     'L0_attn_b_Wproj': 8.0}
    for name, (base, spread) in spreads.items():
        noise = np.random.default_rng([zlib.crc32(name.encode()), seed]).standard_normal(out[name].shape)
        drawn = base * np.exp(spread * noise) if base else spread * noise
        out[name] = jnp.asarray(drawn.astype(out[name].dtype))
    for name, factor in factors.items():
        out[name] = (out[name] * factor).astype(out[name].dtype)
    return out
```

```python
import concourse.bass as bass
from concourse import mybir
from contextlib import ExitStack

fp32 = mybir.dt.float32
fp16 = mybir.dt.float16
bf16 = mybir.dt.bfloat16
i32 = mybir.dt.int32
u32 = mybir.dt.uint32
ALU = mybir.AluOpType
ACT = mybir.ActivationFunctionType
AX = mybir.AxisListType

P = 128
B, S, D = 2, 2048, 256
N = B * S
TILES = N // P
SEQ_TILES = S // P
C = D // P
H = 16
HD = D // H
E = 8
F = 256
FC = F // P
CAP = N // E
EPS_LN = 1e-5
EPS_DEN = 1e-6
BIG = 1e30
ROW = D + E
WINDOWS = [max(4, 256 // 2 ** h) for h in range(H)]
REACH = [min(P, w) for w in WINDOWS]
REACH_AT = [sum(REACH[:h]) for h in range(H)]
REACH_ALL = sum(REACH)
BISECTIONS = 28
GROUPS = P // E
GT = N // GROUPS
SLOT_HI, SLOT_LO = 32, CAP // 32
PLACED = 107


def later(t, n):
    return not isinstance(t, int) or t >= n


def active(t):
    return not isinstance(t, int) or 0 <= t < TILES


def pipeline(eng, slot, first, lo, hi, last, unroll):
    assert (hi - lo) % unroll == 0
    for i in range(first, lo):
        slot(i, i % unroll)
    with eng.Fori(0, (hi - lo) // unroll) as n:
        for u in range(unroll):
            slot(n * unroll + (lo + u), (lo + u) % unroll)
    for i in range(hi, last + 1):
        slot(i, i % unroll)


def head(g, j):
    return 8 * (g // 2) + 2 * j + g % 2


def tied(parity):
    strips, at = [], 0
    for back, h in [(2, 0)] * (parity == 0) + [(1, h) for h in range(parity, H, 2)]:
        strips.append((h, back, REACH[h], at))
        at += REACH[h]
    return strips, at


def place_of(h):
    return 8 * (h // 8) + 4 * (h % 2) + (h % 8) // 2


TIED = [tied(0), tied(1)]
TIED_AT = [0, TIED[0][1]]
TIED_ALL = TIED[0][1] + TIED[1][1]


class Core:

    def __init__(self, nc, ctx):
        self.nc, self.ctx = nc, ctx
        self.x = self.sb("x_sb", [P, TILES, D], fp32)
        self.logits = self.sb("logits_sb", [P, TILES, E], fp32)
        self.bank = [self.ps(f"bank{i}") for i in range(8)]
        self.ident = self.sb("ident", [P, P], fp32)
        self.ident16 = self.sb("ident16", [P, P], fp16)
        self.identb = self.sb("identb", [P, P], bf16)
        self.half = self.sb("half", [P, 1], fp32)
        self.eps = self.sb("eps", [P, 1], fp32)
        self.wg = self.sb("wg", [P, C, E], fp32)
        self.mask_q = self.sb("mask_q", [P, 4, 4, P], bf16)
        self.mask_k = self.sb("mask_k", [P, 4, 4, P], bf16)
        self.tied_q = self.sb("tied_q", [P, TIED_ALL], bf16)
        self.tied_k = self.sb("tied_k", [P, TIED_ALL], bf16)

    def sb(self, name, shape, dt):
        return self.ctx.enter_context(self.nc.sbuf_tensor(name, shape, dt))

    def ps(self, name):
        return self.ctx.enter_context(self.nc.psum_tensor(name, [P, 512], fp32))


def setup(nc, k, gate_wt):
    with ExitStack() as ctx:
        zeroed = nc.alloc_semaphore("zeroed")
        ready = nc.alloc_semaphore("ident_ready")
        copied = nc.alloc_semaphore("ident_copied")
        loaded = nc.alloc_semaphore("wg_loaded")
        with nc.Block() as block:
            @block.sync
            def _(sp):
                sp.dma_start(k.wg[:, :, :], gate_wt.rearrange("(c p) e -> p c e", p=P)).then_inc(loaded, 16)
                sp.wait_ge(loaded, 16)

            @block.gpsimd
            def _(pool):
                pool.memset(k.ident[:, :], 0.0).then_inc(zeroed, 1)
                pool.memset(k.half[:, :], -0.5).then_inc(zeroed, 1)
                pool.memset(k.eps[:, :], EPS_LN).then_inc(zeroed, 1)
                pool.wait_ge(zeroed, 3)
                pool.affine_select(out=k.ident[:, :], in_=k.ident[:, :], compare_op=ALU.not_equal, fill=1.0,
                                   base=0, pattern=[[-1, P]], channel_multiplier=1).then_inc(ready, 1)

            @block.vector
            def _(dve):
                dve.wait_ge(ready, 1)
                dve.tensor_copy(k.ident16[:, :], k.ident[:, :]).then_inc(copied, 1)
                dve.tensor_copy(k.identb[:, :], k.ident[:, :]).then_inc(copied, 1)
                dve.wait_ge(copied, 2)


def window_masks(k, pool, fill):
    for m in (k.mask_q[:, :, :, :], k.mask_k[:, :, :, :], k.tied_q[:, :], k.tied_k[:, :]):
        pool.memset(m, 0.0).then_inc(fill, 1)
    pool.wait_ge(fill, 4)
    done = 4

    def select(m, base, mult, step):
        nonlocal done
        pool.affine_select(out=m, in_=m, compare_op=ALU.is_ge, fill=-BIG, base=base,
                           pattern=[[step, m.shape[-1]]], channel_multiplier=mult).then_inc(fill, 1)
        done += 1
    for g in range(4):
        for j in range(4):
            select(k.mask_q[:, g, j, :], 0, 1, -1)
            select(k.mask_k[:, g, j, :], 0, -1, 1)
    pool.wait_ge(fill, done)
    for g in range(4):
        for j in range(4):
            wd = WINDOWS[head(g, j)]
            if wd < P:
                select(k.mask_q[:, g, j, :], wd - 1, -1, 1)
                select(k.mask_k[:, g, j, :], wd - 1, 1, -1)
    for s in range(2):
        for h, back, n, at in TIED[s][0]:
            a = TIED_AT[s] + at
            select(k.tied_q[:, a:a + n], WINDOWS[h] - 1 - back * P + (P - n), -1, 1)
            select(k.tied_k[:, a:a + n], WINDOWS[h] - 1 - back * P, 1, -1)
    pool.wait_ge(fill, done)



def linear_attention(nc, k, x_in, wq, wk, wv, wo, x_base, rows):
    with ExitStack() as ctx:
        def sb(name, shape, dt=fp32):
            return ctx.enter_context(nc.sbuf_tensor("la_" + name, shape, dt))

        def sem(name):
            return nc.alloc_semaphore("la_" + name)

        w = sb("w", [P, C, 3 * D])
        w_o = sb("wo", [P, C, D])
        causal = sb("causal", [P, P])
        diag = sb("diag", [P, C, E, HD + 1])
        keep = sb("keep", [P, TILES])
        state = sb("state", [P, C, E, 2 * HD])
        kv = sb("kv", [P, C, E, HD + 1])
        stats, mv, veps, rstd = (sb(n, [P, 2, 6]) for n in ("stats", "mv", "veps", "rstd"))
        stats2, mv2, veps2, rstd2 = (sb(n, [P, 2, 6]) for n in ("stats2", "mv2", "veps2", "rstd2"))
        xn = sb("xn", [P, 2, D])
        xT = sb("xT", [P, 2, C, P])
        ex = sb("ex", [P, 2, 2 * D])
        relu = sb("relu", [P, 2, 2 * D])
        v1 = sb("v1", [P, 2, H, 2 * HD])
        qk = sb("qk", [P, 2, 2 * D])
        stack = sb("stack", [P, 2, 2, H, 4, HD], fp16)
        qS = sb("qS", [P, 2, H // 2, P], fp16)
        kS = sb("kS", [P, 2, H // 2, P], fp16)
        qT = sb("qT", [P, 2, C, P])
        sc = sb("sc", [P, 4, 4, P])
        outT = sb("outT", [P, 2, 4, P])
        den = sb("den", [P, 2, H])
        rden = sb("rden", [P, 2, H])
        o = sb("o", [P, 2, H, HD])
        oT = sb("oT", [P, 2, C, P])
        x1 = sb("x1", [P, 2, D])
        xn2 = sb("xn2", [P, 2, D])
        x2T = sb("x2T", [P, 2, C, P])

        (w_loaded, consts, cfill, dfill, x_first, x_loaded) = (sem(n) for n in (
            "w_loaded", "consts", "cfill", "dfill", "x_first", "x_loaded"))
        (stats_d, mv_d, veps_d, rstd_d, xn_d, xT_p, xT_d, qk_p, v_p, ex_d, relu_d, v_d, feat_d, hi_d, lo_d,
         qS_p, kS_p, qT_p, qS_d, kS_d, qT_d, sc_p, sc_d, out_p, outT_d, o2_p, den_d, rden_d, o_d,
         oT_p, oT_d, y_p, x1_d, kv_p, kvm_d, state_d, stats2_d, mv2_d, veps2_d, rstd2_d, xn2_d,
         x2T_p, x2T_d, lg_p, lg_d, x1_s, xn2_s) = (sem(n) for n in (
            "stats_d", "mv_d", "veps_d", "rstd_d", "xn_d", "xT_p", "xT_d", "qk_p", "v_p", "ex_d", "relu_d",
            "v_d", "feat_d", "hi_d", "lo_d", "qS_p", "kS_p", "qT_p", "qS_d", "kS_d", "qT_d", "sc_p", "sc_d",
            "out_p", "outT_d", "o2_p", "den_d", "rden_d", "o_d", "oT_p", "oT_d", "y_p", "x1_d", "kv_p",
            "kvm_d", "state_d", "stats2_d", "mv2_d", "veps2_d", "rstd2_d", "xn2_d", "x2T_p", "x2T_d",
            "lg_p", "lg_d", "x1_s", "xn2_s"))
        X, QK, V, TQ, TK, S0, S1, O = k.bank
        SC = [S0, S1]
        XCHUNK = 4

        with nc.Block() as block:
            @block.sync
            def _(sp):
                x_view = x_in.rearrange("(t p) d -> p t d", p=P)
                for g in range(TILES // XCHUNK):
                    sp.dma_start(k.x[:, g * XCHUNK:(g + 1) * XCHUNK, :],
                                 x_view[:, g * XCHUNK:(g + 1) * XCHUNK, :]).then_inc(x_first if g == 0 else x_loaded, 16)
                    if g == 0:
                        for n, wx in enumerate((wq, wk, wv)):
                            sp.dma_start(w[:, :, n * D:(n + 1) * D],
                                         wx.rearrange("(c p) n -> p c n", p=P)).then_inc(w_loaded, 16)
                        sp.dma_start(w_o[:, :, :], wo.rearrange("(c p) n -> p c n", p=P)).then_inc(w_loaded, 16)

                def slot(i, p):
                    t, q = i - 1, (p + 1) % 2
                    if active(t):
                        sp.wait_ge(x1_d, t + 1)
                        sp.dma_start(x_base[bass.ds(t * P, P), :], x1[:, q, :]).then_inc(x1_s, 16)
                        sp.wait_ge(xn2_d, t + 1)
                        sp.dma_start(rows[bass.ds(t * P, P), 0:D], xn2[:, q, :]).then_inc(xn2_s, 16)
                pipeline(sp, slot, 1, 4, 30, 32, 2)
                sp.wait_ge(w_loaded, 64)
                sp.wait_ge(x1_s, 16 * TILES)
                sp.wait_ge(xn2_s, 16 * TILES)

            @block.gpsimd
            def _(pool):
                pool.memset(causal[:, :], 1.0).then_inc(cfill, 1)
                pool.memset(diag[:, :, :, :], 1.0).then_inc(cfill, 1)
                pool.wait_ge(cfill, 2)
                pool.affine_select(out=causal[:, :], in_=causal[:, :], compare_op=ALU.is_ge, fill=0.0,
                                   base=0, pattern=[[1, P]], channel_multiplier=-1).then_inc(cfill, 1)
                halves = diag[:, 0, :, :].rearrange("p (b j) n -> p b j n", b=2)
                pool.affine_select(out=halves, in_=halves, compare_op=ALU.is_ge, fill=0.0,
                                   base=0, pattern=[[-HD, 2], [-2 * HD, 4], [0, HD + 1]],
                                   channel_multiplier=1).then_inc(cfill, 1)
                pool.wait_ge(cfill, 4)
                pool.affine_select(out=halves, in_=halves, compare_op=ALU.is_ge, fill=0.0,
                                   base=HD - 1, pattern=[[HD, 2], [2 * HD, 4], [0, HD + 1]],
                                   channel_multiplier=-1).then_inc(cfill, 1)
                pool.wait_ge(cfill, 5)
                pool.tensor_copy(diag[:, 1, :, :], diag[:, 0, :, :]).then_inc(consts, 1)

                def slot(i, p):
                    t, q = i + 2, p
                    if active(t):
                        pool.wait_ge(mv_d, t + 1)
                        pool.tensor_tensor(veps[:, q, 0:1], mv[:, q, 1:2], k.eps[:, :], ALU.add).then_inc(veps_d, 1)
                        pool.wait_ge(veps_d, t + 1)
                        pool.tensor_tensor(rstd[:, q, 0:1], veps[:, q, 0:1], k.half[:, :], ALU.pow).then_inc(rstd_d, 1)
                    t, q = i - 1, (p + 1) % 2
                    if active(t):
                        pool.wait_ge(mv2_d, t + 1)
                        pool.tensor_tensor(veps2[:, q, 0:1], mv2[:, q, 1:2], k.eps[:, :], ALU.add).then_inc(veps2_d, 1)
                        pool.wait_ge(veps2_d, t + 1)
                        pool.tensor_tensor(rstd2[:, q, 0:1], veps2[:, q, 0:1], k.half[:, :], ALU.pow).then_inc(rstd2_d, 1)
                pipeline(pool, slot, -2, 4, 30, 32, 2)

            @block.vector
            def _(dve):
                dve.memset(state[:, :, :, :], 0.0).then_inc(dfill, 1)
                dve.memset(keep[:, :], 1.0).then_inc(dfill, 1)
                dve.memset(v1[:, :, :, :], 1.0).then_inc(dfill, 1)
                dve.memset(stack[:, :, :, :, :, :], 0.0).then_inc(dfill, 1)
                dve.wait_ge(dfill, 4)
                dve.memset(keep[:, SEQ_TILES - 1:SEQ_TILES], 0.0).then_inc(consts, 1)
                dve.wait_ge(consts, 2)

                def slot(i, p):
                    t, q = i, p
                    if active(t):
                        for g in (0, 1):
                            masked_scores(t, g)
                    t, q = i - 1, (p + 1) % 2
                    if active(t):
                        o2 = TQ[:, :].rearrange("p (h c) -> p h c", h=H)
                        dve.wait_ge(o2_p, t + 1)
                        dve.tensor_scalar(den[:, q, :], o2[:, :, HD], EPS_DEN, None, ALU.add).then_inc(den_d, 1)
                        dve.wait_ge(den_d, t + 1)
                        dve.reciprocal(rden[:, q, :], den[:, q, :]).then_inc(rden_d, 1)
                        dve.wait_ge(rden_d, t + 1)
                        dve.tensor_tensor(o[:, q, :, :], o2[:, :, 0:HD],
                                          rden[:, q, :].unsqueeze(2).broadcast_to([P, H, HD]), ALU.mult).then_inc(o_d, 1)
                    t, q = i, p
                    if active(t):
                        masked_scores(t, 2)
                    t, q = i + 1, (p + 1) % 2
                    if active(t):
                        dve.wait_ge(relu_d, t + 1)
                        if later(t, 2):
                            dve.wait_ge(kv_p, t - 1)
                            dve.wait_ge(qT_p, t - 1)
                        dve.scalar_tensor_tensor(qk[:, q, :], ex[:, q, :], 1.0, relu[:, q, :], ALU.min,
                                                 ALU.add).then_inc(feat_d, 1)
                        dve.wait_ge(feat_d, t + 1)
                        if later(t, 2):
                            dve.wait_ge(qS_p, t - 1)
                            dve.wait_ge(kS_p, t - 1)
                        qv = qk[:, q, :].rearrange("p (n h d) -> p n h d", n=2, h=H)
                        dve.tensor_copy(stack[:, q, 0, :, 0:2, :],
                                        qv[:, 0, :, :].unsqueeze(2).broadcast_to([P, H, 2, HD])).then_inc(hi_d, 1)
                        dve.tensor_copy(stack[:, q, 1, :, 0:3:2, :],
                                        qv[:, 1, :, :].unsqueeze(2).broadcast_to([P, H, 2, HD])).then_inc(hi_d, 1)
                        dve.wait_ge(hi_d, (t + 1) * 2)
                        dve.tensor_tensor(stack[:, q, 0, :, 2, :], qv[:, 0, :, :], stack[:, q, 0, :, 0, :],
                                          ALU.subtract).then_inc(lo_d, 1)
                        dve.tensor_tensor(stack[:, q, 1, :, 1, :], qv[:, 1, :, :], stack[:, q, 1, :, 0, :],
                                          ALU.subtract).then_inc(lo_d, 1)
                    t, q = i, p
                    if active(t):
                        masked_scores(t, 3)
                        dve.wait_ge(kv_p, t + 1)
                        kvp = V[:, 0:C * E * (HD + 1)].rearrange("p (c h n) -> p (c h) n", c=C, h=E)
                        dve.scalar_tensor_tensor(kv[:, :, :, :].rearrange("p c h n -> p (c h) n"), kvp,
                                                 keep[:, bass.ds(t, 1)],
                                                 diag[:, :, :, :].rearrange("p c h n -> p (c h) n"),
                                                 ALU.mult, ALU.mult).then_inc(kvm_d, 1)
                        dve.wait_ge(kvm_d, t + 1)
                        dve.wait_ge(out_p, t + 1)
                        sv = state[:, :, :, 0:HD + 1].rearrange("p c h n -> p (c h) n")
                        dve.scalar_tensor_tensor(sv, sv, keep[:, bass.ds(t, 1)],
                                                 kv[:, :, :, :].rearrange("p c h n -> p (c h) n"),
                                                 ALU.mult, ALU.add).then_inc(state_d, 1)
                    t, q = i - 1, (p + 1) % 2
                    if active(t):
                        if later(t, 1):
                            dve.wait_ge(x1_s, t * 16)
                        dve.wait_ge(y_p, t + 1)
                        dve.tensor_tensor(x1[:, q, :], X[:, 0:D],
                                          k.x[:, bass.ds(t, 1), :].squeeze(1), ALU.add).then_inc(x1_d, 1)
                        dve.wait_ge(x1_d, t + 1)
                        dve.bn_stats(stats2[:, q, 0:6], x1[:, q, :]).then_inc(stats2_d, 1)
                    t, q = i + 2, p
                    if active(t):
                        dve.wait_ge(x_first, 16)
                        if later(t, XCHUNK):
                            dve.wait_ge(x_loaded, 16 * (TILES // XCHUNK - 1))
                        dve.bn_stats(stats[:, q, 0:6], k.x[:, bass.ds(t, 1), :].squeeze(1)).then_inc(stats_d, 1)
                    if active(i + 2):
                        dve.wait_ge(stats_d, i + 3)
                    if active(i - 1):
                        dve.wait_ge(stats2_d, i)
                    t, q = i + 1, (p + 1) % 2
                    if active(t):
                        dve.wait_ge(kS_p, t + 1)
                        dve.tensor_copy(kS[:, q, :, :], TK[:, :].bitcast(fp16).rearrange("p (h t) -> p h t", t=P)).then_inc(kS_d, 1)
                    t, q = i - 1, (p + 1) % 2
                    if active(t):
                        dve.bn_aggr(mv2[:, q, 0:2], stats2[:, q, 0:6]).then_inc(mv2_d, 1)
                    t, q = i + 2, p
                    if active(t):
                        dve.bn_aggr(mv[:, q, 0:2], stats[:, q, 0:6]).then_inc(mv_d, 1)
                        dve.wait_ge(rstd_d, t + 1)
                        dve.wait_ge(mv_d, t + 1)
                        if later(t, 2):
                            dve.wait_ge(xT_p, t - 1)
                        dve.tensor_scalar(xn[:, q, :], k.x[:, bass.ds(t, 1), :].squeeze(1), mv[:, q, 0:1],
                                          rstd[:, q, 0:1], ALU.subtract, ALU.mult).then_inc(xn_d, 1)
                    t, q = i - 1, (p + 1) % 2
                    if active(t):
                        dve.wait_ge(rstd2_d, t + 1)
                        dve.wait_ge(mv2_d, t + 1)
                        if later(t, 2):
                            dve.wait_ge(x2T_p, t - 1)
                        if later(t, 1):
                            dve.wait_ge(xn2_s, t * 16)
                        dve.tensor_scalar(xn2[:, q, :], x1[:, q, :], mv2[:, q, 0:1],
                                          rstd2[:, q, 0:1], ALU.subtract, ALU.mult).then_inc(xn2_d, 1)

                def masked_scores(t, g):
                    dve.wait_ge(sc_p, t * 4 + (g + 1))
                    if later(t, 1):
                        dve.wait_ge(out_p, t)
                    dve.tensor_tensor(sc[:, g, :, :], SC[g % 2][:, :].rearrange("p (h t) -> p h t", t=P),
                                      causal[:, :].unsqueeze(1).broadcast_to([P, 4, P]), ALU.mult).then_inc(sc_d, 1)

                pipeline(dve, slot, -2, 4, 30, 32, 2)

            @block.scalar
            def _(act):
                act.wait_ge(consts, 2)

                def slot(i, p):
                    t, q = i + 1, (p + 1) % 2
                    if active(t):
                        act.wait_ge(xT_p, t + 1)
                        if later(t, 2):
                            act.wait_ge(v_p, t - 1)
                        act.activation(xT[:, q, :, :], X[:, 0:D].rearrange("p (c t) -> p c t", c=C), ACT.Copy).then_inc(xT_d, 1)
                        act.wait_ge(qk_p, t + 1)
                        if later(t, 2):
                            act.wait_ge(feat_d, t - 1)
                        act.activation(ex[:, q, :], QK[:, :], ACT.Exp).then_inc(ex_d, 1)
                        act.activation(relu[:, q, :], QK[:, :], ACT.Relu).then_inc(relu_d, 1)
                        act.wait_ge(v_p, t + 1)
                        if later(t, 2):
                            act.wait_ge(kv_p, t - 1)
                            act.wait_ge(out_p, t - 1)
                        act.activation(v1[:, q, :, 0:HD], V[:, 0:D].rearrange("p (h d) -> p h d", h=H), ACT.Copy).then_inc(v_d, 1)
                    t, q = i - 1, (p + 1) % 2
                    if active(t):
                        act.wait_ge(oT_p, t + 1)
                        if later(t, 2):
                            act.wait_ge(y_p, t - 1)
                        act.activation(oT[:, q, :, :], X[:, 0:D].rearrange("p (c t) -> p c t", c=C), ACT.Copy).then_inc(oT_d, 1)
                    t, q = i, p
                    if active(t):
                        act.wait_ge(out_p, t + 1)
                        if later(t, 2):
                            act.wait_ge(o2_p, t - 1)
                        act.activation(outT[:, q, :, :], O[:, :].rearrange("p (g t) -> p g t", g=4), ACT.Copy).then_inc(outT_d, 1)
                    t, q = i - 2, p
                    if active(t):
                        act.wait_ge(x2T_p, t + 1)
                        if later(t, 2):
                            act.wait_ge(lg_p, t - 1)
                        act.activation(x2T[:, q, :, :], X[:, 0:D].rearrange("p (c t) -> p c t", c=C), ACT.Copy).then_inc(x2T_d, 1)
                    t, q = i + 1, (p + 1) % 2
                    if active(t):
                        act.wait_ge(qS_p, t + 1)
                        if later(t, 2):
                            act.wait_ge(out_p, t - 1)
                        act.activation(qS[:, q, :, :], TQ[:, :].bitcast(fp16).rearrange("p (h t) -> p h t", t=P), ACT.Copy).then_inc(qS_d, 1)
                        act.wait_ge(qT_p, t + 1)
                        act.activation(qT[:, q, :, :], V[:, 0:D].rearrange("p (c t) -> p c t", c=C), ACT.Copy).then_inc(qT_d, 1)
                    t, q = i - 2, p
                    if active(t):
                        act.wait_ge(lg_p, t + 1)
                        act.activation(k.logits[:, bass.ds(t, 1), :].squeeze(1), X[:, 0:E], ACT.Copy).then_inc(lg_d, 1)
                pipeline(act, slot, -1, 4, 30, 33, 2)

            @block.tensor
            def _(pe):
                pe.wait_ge(w_loaded, 64)
                pe.wait_ge(consts, 2)

                def transpose2(bank, src, done):
                    for c in range(C):
                        last = pe.transpose(bank[:, c * P:(c + 1) * P], src[:, c * P:(c + 1) * P], k.ident[:, :])
                    last.then_inc(done, 1)

                def scores(t, q, g):
                    if g < 2:
                        if later(t, 1):
                            pe.wait_ge(sc_d, t * 4 + (g - 1))
                    else:
                        pe.wait_ge(sc_d, t * 4 + (g - 1))
                    r = 64 * (g % 2)
                    for j in range(4):
                        h = head(g, j)
                        last = pe.matmul(SC[g % 2][:, j * P:(j + 1) * P], kS[r:r + 64, q, h // 2, :],
                                         qS[r:r + 64, q, h // 2, :], start=True, stop=True)
                    last.then_inc(sc_p, 1)

                def attend(t, q, g):
                    pe.wait_ge(sc_d, t * 4 + (g + 1))
                    for j in range(4):
                        last = pe.matmul(O[32 * j:32 * j + 32, g * P:(g + 1) * P], v1[:, q, 4 * g + j, :],
                                         sc[:, g, j, :], start=False, stop=True, skip_group_check=True)
                    return last

                def slot(i, p):
                    t, q = i, p
                    if active(t):
                        pe.wait_ge(qS_d, t + 1)
                        pe.wait_ge(kS_d, t + 1)
                        scores(t, q, 0)
                        scores(t, q, 1)
                    t, q = i + 1, (p + 1) % 2
                    if active(t):
                        pe.wait_ge(xn_d, t + 1)
                        if later(t, 4):
                            pe.wait_ge(lg_d, t - 3)
                        elif t == 3:
                            pe.wait_ge(x1_d, 1)
                        elif t > 0:
                            pe.wait_ge(xT_d, t)
                        transpose2(X, xn[:, q, :], xT_p)
                    t, q = i - 1, (p + 1) % 2
                    if active(t):
                        pe.wait_ge(outT_d, t + 1)
                        if active(i):
                            pe.wait_ge(qS_d, t + 2)
                        else:
                            pe.wait_ge(o_d, t)
                        for g in range(4):
                            last = pe.transpose(TQ[:, g * P:(g + 1) * P], outT[:, q, g, :], k.ident[:, :])
                        last.then_inc(o2_p, 1)
                    t, q = i, p
                    if active(t):
                        pe.wait_ge(qT_d, t + 1)
                        pe.wait_ge(v_d, t + 1)
                        if later(t, 1):
                            pe.wait_ge(state_d, t)
                            pe.wait_ge(outT_d, t)
                        for g in range(4):
                            pe.matmul(O[:, g * P:(g + 1) * P], state[:, g // 2, 4 * (g % 2):4 * (g % 2) + 4, :].rearrange("p h n -> p (h n)"),
                                      qT[:, q, g // 2, :], start=(g == 0), stop=True, skip_group_check=True)
                        attend(t, q, 0)
                        scores(t, q, 2)
                    t, q = i + 1, (p + 1) % 2
                    if active(t):
                        pe.wait_ge(xT_d, t + 1)
                        if later(t, 1):
                            pe.wait_ge(relu_d, t)
                            pe.wait_ge(qT_d, t)
                        for c in range(C):
                            last = pe.matmul(QK[:, :], xT[:, q, c, :], w[:, c, 0:2 * D], start=(c == 0), stop=(c == C - 1))
                        last.then_inc(qk_p, 1)
                        for c in range(C):
                            last = pe.matmul(V[:, 0:D], xT[:, q, c, :], w[:, c, 2 * D:3 * D], start=(c == 0), stop=(c == C - 1))
                        last.then_inc(v_p, 1)
                    t, q = i, p
                    if active(t):
                        attend(t, q, 1)
                        scores(t, q, 3)
                    t, q = i - 1, (p + 1) % 2
                    if active(t):
                        pe.wait_ge(o_d, t + 1)
                        if active(i + 1):
                            pe.wait_ge(xT_d, t + 3)
                        else:
                            pe.wait_ge(lg_d, t - 1)
                        transpose2(X, o[:, q, :, :].rearrange("p h d -> p (h d)"), oT_p)
                    t, q = i, p
                    if active(t):
                        if active(i + 1):
                            pe.wait_ge(v_d, t + 2)
                        for c in range(C):
                            last = pe.matmul(V[:, c * E * (HD + 1):(c + 1) * E * (HD + 1)].rearrange("p (h n) -> p h n", h=E),
                                             qk[:, q, D + c * P:D + (c + 1) * P],
                                             v1[:, q, c * E:(c + 1) * E, 0:HD + 1], start=True, stop=True)
                        last.then_inc(kv_p, 1)
                        attend(t, q, 2)
                    t, q = i - 1, (p + 1) % 2
                    if active(t):
                        pe.wait_ge(oT_d, t + 1)
                        for c in range(C):
                            last = pe.matmul(X[:, 0:D], oT[:, q, c, :], w_o[:, c, :], start=(c == 0), stop=(c == C - 1))
                        last.then_inc(y_p, 1)
                    t, q = i, p
                    if active(t):
                        attend(t, q, 3).then_inc(out_p, 1)
                    t, q = i - 2, p
                    if active(t):
                        pe.wait_ge(xn2_d, t + 1)
                        if active(i - 1):
                            pe.wait_ge(x1_d, t + 2)
                        else:
                            pe.wait_ge(lg_d, t)
                        transpose2(X, xn2[:, q, :], x2T_p)
                    t, q = i + 1, (p + 1) % 2
                    if active(t):
                        pe.wait_ge(lo_d, (t + 1) * 2)
                        if later(t, 2):
                            pe.wait_ge(o_d, t - 1)
                        elif t == 1:
                            pe.wait_ge(qS_d, 1)
                        for h in range(H // 2):
                            last = pe.transpose(TQ[:, :].bitcast(fp16)[:, h * P:(h + 1) * P],
                                                stack[:, q, 0, 2 * h:2 * h + 2, :, :].rearrange("p h n d -> p (h n d)"), k.ident16[:, :])
                        last.then_inc(qS_p, 1)
                        if later(t, 1):
                            pe.wait_ge(kS_d, t)
                        for h in range(H // 2):
                            last = pe.transpose(TK[:, :].bitcast(fp16)[:, h * P:(h + 1) * P],
                                                stack[:, q, 1, 2 * h:2 * h + 2, :, :].rearrange("p h n d -> p (h n d)"), k.ident16[:, :])
                        last.then_inc(kS_p, 1)
                        if later(t, 1):
                            pe.wait_ge(kvm_d, t)
                        else:
                            pe.wait_ge(v_d, 1)
                        transpose2(V, qk[:, q, 0:D], qT_p)
                    t, q = i - 2, p
                    if active(t):
                        pe.wait_ge(x2T_d, t + 1)
                        for c in range(C):
                            last = pe.matmul(X[:, 0:E], x2T[:, q, c, :], k.wg[:, c, :], start=(c == 0), stop=(c == C - 1))
                        last.then_inc(lg_p, 1)
                pipeline(pe, slot, -1, 4, 30, 33, 2)



def router(nc, k, name, rows, lists, masks):
    THRESHOLD = 0.9
    OUTSIDE = -16.0
    FAR = float(N)
    with ExitStack() as ctx:
        def sb(n, shape, dt=fp32):
            return ctx.enter_context(nc.sbuf_tensor(f"{name}_{n}", shape, dt))

        def sem(n):
            return nc.alloc_semaphore(f"{name}_{n}")

        block16 = sb("block16", [P, P], bf16)
        before16 = sb("before16", [P, P], bf16)
        token = sb("token", [P, 2, E, GROUPS], fp16)
        token_i = sb("token_i", [P, 2, E, GROUPS], i32)
        mx = sb("mx", [P, TILES])
        shifted = sb("shifted", [P, TILES, E])
        exps = sb("exps", [P, TILES, E])
        total = sb("total", [P, TILES])
        inv = sb("inv", [P, TILES])
        prob = sb("prob", [P, TILES, E])
        ahead = sb("ahead", [P, TILES, E, E])
        mass = sb("mass", [P, TILES, E, E])
        rank = sb("rank", [P, TILES, E])
        ahead_sum = sb("ahead_sum", [P, TILES, E])
        chosen = sb("chosen", [P, TILES, E])
        gap = sb("gap", [P, TILES, E])
        outside = sb("outside", [P, TILES, E])
        score = sb("score", [P, TILES, E])
        key_t = sb("key_t", [P, 2, E, GROUPS])
        key = sb("key", [P, GT])
        hits = sb("hits", [P, GT], bf16)
        count = sb("count", [P, 1], bf16)
        floor, cand, gain = (sb(n, [P, 1]) for n in ("floor", "cand", "gain"))
        step = sb("step", [P, 2])
        above = sb("above", [P, GT])
        equal = sb("equal", [P, GT])
        zeros = sb("zeros", [P, GT])
        scan = sb("scan", [P, GT])
        need = sb("need", [P, 1])
        offset = sb("offset", [P, 2])
        ties = sb("ties", [P, GT])
        kept = sb("kept", [P, GT])
        place = sb("place", [P, GT])
        place_t = sb("place_t", [P, GT], i32)
        parts = sb("parts", [P, 2, GT], i32)
        hi = sb("hi", [P, GT], fp16)
        lo = sb("lo", [P, GT], fp16)
        is_hi = sb("is_hi", [P, SLOT_HI, GT], fp16)
        lo_token = sb("lo_token", [P, SLOT_LO, GT], fp16)
        listed = sb("listed", [SLOT_HI, E * SLOT_LO], i32)

        v, fill, consts, exps_d, key_p, count_d, sum_p, place_p, onehot_d, list_p, score_s, list_s, keyt_d, placed = (
            sem(n) for n in ("v", "fill", "consts", "exps_d", "key_p", "count_d", "sum_p", "place_p", "onehot_d",
                             "list_p", "score_s", "list_s", "keyt_d", "placed"))
        shift_d, score_d, masks_d = sem("shift_d"), sem("score_d"), sem("masks_d")
        KEY, SUM, PLACE, LIST = k.bank[0:4]
        by_tile = "p j e t -> p t j e"

        with nc.Block() as block:
            @block.gpsimd
            def _(pool):
                pool.memset(block16[:, :], 1.0).then_inc(fill, 1)
                pool.memset(before16[:, :], 1.0).then_inc(fill, 1)
                pool.iota(token_i[:, :, :, :], pattern=[[P, 2], [0, E], [2 * P, GROUPS]], base=-(N // 2),
                          channel_multiplier=1).then_inc(fill, 1)
                pool.wait_ge(fill, 3)
                for n, m in enumerate((block16, before16)):
                    mv = m[:, :].rearrange("p (e g) -> p e g", e=E)
                    pool.affine_select(out=mv, in_=mv, compare_op=ALU.is_ge, fill=0.0, base=0,
                                       pattern=[[-GROUPS, E], [0, GROUPS]], channel_multiplier=1).then_inc(fill, 1)
                    pool.wait_ge(fill, 4 + 2 * n)
                    if n == 0:
                        pool.affine_select(out=mv, in_=mv, compare_op=ALU.is_ge, fill=0.0, base=GROUPS - 1,
                                           pattern=[[GROUPS, E], [0, GROUPS]], channel_multiplier=-1).then_inc(fill, 1)
                    else:
                        pool.affine_select(out=mv, in_=mv, compare_op=ALU.is_gt, fill=0.0, base=0,
                                           pattern=[[GROUPS, E], [1, GROUPS]], channel_multiplier=-1).then_inc(fill, 1)
                    pool.wait_ge(fill, 5 + 2 * n)
                pool.tensor_copy(token[:, :, :, :], token_i[:, :, :, :]).then_inc(consts, 1)
                if masks:
                    window_masks(k, pool, masks_d)

            @block.sync
            def _(sp):
                sp.wait_ge(score_d, 1)
                sp.dma_start(rows[:, D:ROW].rearrange("(t p) e -> p t e", p=P), score[:, :, :]).then_inc(score_s, 16)
                sp.wait_ge(placed, 1)
                sp.dma_start(lists.rearrange("e (h l) -> h e l", h=SLOT_HI),
                             listed[:, :].rearrange("h (e l) -> h e l", e=E)).then_inc(list_s, 16)
                sp.wait_ge(list_s, 16)
                sp.wait_ge(score_s, 16)

            @block.scalar
            def _(act):
                act.wait_ge(shift_d, 1)
                act.activation(exps[:, :, :], shifted[:, :, :], ACT.Exp).then_inc(exps_d, 1)

            @block.tensor
            def _(pe):
                pe.wait_ge(keyt_d, 1)
                for j in range(2):
                    last = pe.transpose(KEY[:, j * P:(j + 1) * P], key_t[:, j, :, :].rearrange("p e t -> p (e t)"), k.ident[:, :])
                last.then_inc(key_p, 1)
                pe.wait_ge(consts, 1)
                with pe.Fori(0, BISECTIONS // 2) as n:
                    for u in range(2):
                        pe.wait_ge(count_d, n * 2 + (u + 1))
                        pe.matmul(SUM[:, 0:1], block16[:, :], count[:, :], start=True, stop=True).then_inc(sum_p, 1)
                pe.wait_ge(count_d, BISECTIONS + 1)
                pe.matmul(SUM[:, 0:1], block16[:, :], count[:, :], start=True, stop=True).then_inc(sum_p, 1)
                for n in (2, 3):
                    pe.wait_ge(count_d, BISECTIONS + n)
                    pe.matmul(SUM[:, 0:1], before16[:, :], count[:, :], start=True, stop=True).then_inc(sum_p, 1)
                pe.wait_ge(v, PLACED)
                for j in range(2):
                    last = pe.transpose(PLACE[:, j * P:(j + 1) * P], place[:, j * P:(j + 1) * P], k.ident[:, :])
                last.then_inc(place_p, 1)
                pe.wait_ge(onehot_d, 1)
                for e in range(E):
                    for n in range(TILES):
                        c = (n // GROUPS) * P + e * GROUPS + n % GROUPS
                        last = pe.matmul(LIST[0:SLOT_HI, e * SLOT_LO:(e + 1) * SLOT_LO], is_hi[:, :, c], lo_token[:, :, c],
                                         start=(n == 0), stop=(n == TILES - 1))
                last.then_inc(list_p, 1)

            @block.vector
            def _(dve):
                done = [0]

                def link(ins):
                    done[0] += 1
                    ins.then_inc(v, 1)
                    dve.wait_ge(v, done[0])

                wide = [P, TILES, E]
                dve.memset(zeros[:, :], 0.0)
                dve.memset(floor[:, :], OUTSIDE)
                dve.memset(cand[:, :], OUTSIDE / 2)
                dve.memset(step[:, 0:1], -OUTSIDE / 2)
                link(dve.memset(ahead[:, :, :, :], 0.0))
                link(dve.reduce_max(mx[:, :], k.logits[:, :, :], AX.X))
                dve.tensor_tensor(shifted[:, :, :], k.logits[:, :, :], mx[:, :].unsqueeze(2).broadcast_to(wide),
                                  ALU.subtract).then_inc(shift_d, 1)
                dve.wait_ge(exps_d, 1)
                link(dve.reduce_sum(total[:, :], exps[:, :, :], AX.X))
                link(dve.reciprocal(inv[:, :], total[:, :]))
                link(dve.tensor_tensor(prob[:, :, :], exps[:, :, :], inv[:, :].unsqueeze(2).broadcast_to(wide), ALU.mult))
                for e in range(E):
                    if e:
                        last = dve.tensor_tensor(ahead[:, :, e, 0:e], prob[:, :, 0:e],
                                                 prob[:, :, e:e + 1].broadcast_to([P, TILES, e]), ALU.is_ge)
                    if e < E - 1:
                        last = dve.tensor_tensor(ahead[:, :, e, e + 1:E], prob[:, :, e + 1:E],
                                                 prob[:, :, e:e + 1].broadcast_to([P, TILES, E - 1 - e]), ALU.is_gt)
                link(last)
                dve.reduce_sum(rank[:, :, :], ahead[:, :, :, :], AX.X)
                link(dve.tensor_tensor(mass[:, :, :, :], ahead[:, :, :, :],
                                       prob[:, :, :].unsqueeze(2).broadcast_to([P, TILES, E, E]), ALU.mult))
                link(dve.reduce_sum(ahead_sum[:, :, :], mass[:, :, :, :], AX.X))
                link(dve.tensor_scalar(chosen[:, :, :], ahead_sum[:, :, :], THRESHOLD, None, ALU.is_lt))
                dve.tensor_tensor(score[:, :, :], prob[:, :, :], chosen[:, :, :], ALU.mult).then_inc(score_d, 1)
                dve.tensor_scalar(outside[:, :, :], chosen[:, :, :], -1.0, -OUTSIDE, ALU.add, ALU.mult)
                link(dve.tensor_scalar(rank[:, :, :], rank[:, :, :], 1.0, None, ALU.add))
                link(dve.tensor_tensor(gap[:, :, :], prob[:, :, :], rank[:, :, :], ALU.subtract))
                link(dve.tensor_tensor(gap[:, :, :], gap[:, :, :], chosen[:, :, :], ALU.mult))
                split = "p (t j) e -> p t j e"
                dve.tensor_tensor(key_t[:, :, :, :].rearrange(by_tile), gap[:, :, :].rearrange(split, j=2),
                                  outside[:, :, :].rearrange(split, j=2), ALU.add).then_inc(keyt_d, 1)
                dve.wait_ge(key_p, 1)
                link(dve.tensor_copy(key[:, :], KEY[:, 0:GT]))
                with dve.Fori(0, BISECTIONS // 2) as n:
                    for u in range(2):
                        at = n * 6 + (done[0] + 3 * u)
                        dve.wait_ge(v, at)
                        dve.tensor_scalar(hits[:, :], key[:, :], cand[:, :], None, ALU.is_ge, ALU.add,
                                          accum_out=count[:, :]).then_inc(count_d, 1)
                        dve.tensor_scalar(step[:, 1 - u:2 - u], step[:, u:u + 1], 0.5, None, ALU.mult)
                        dve.wait_ge(sum_p, n * 2 + (u + 1))
                        dve.tensor_scalar(gain[:, :], SUM[:, 0:1], CAP - 0.5, step[:, u:u + 1], ALU.is_ge,
                                          ALU.mult).then_inc(v, 1)
                        dve.wait_ge(v, at + 1)
                        dve.scalar_tensor_tensor(cand[:, :], gain[:, :], floor[:, :], step[:, 1 - u:2 - u], ALU.add,
                                                 ALU.add).then_inc(v, 1)
                        dve.tensor_tensor(floor[:, :], gain[:, :], floor[:, :], ALU.add).then_inc(v, 1)
                done[0] += 3 * BISECTIONS
                dve.wait_ge(v, done[0])
                dve.tensor_scalar(above[:, :], key[:, :], floor[:, :], None, ALU.is_gt, ALU.add,
                                  accum_out=count[:, :]).then_inc(count_d, 1)
                link(dve.tensor_scalar(equal[:, :], key[:, :], floor[:, :], None, ALU.is_equal))
                link(dve.tensor_tensor_scan(scan[:, :], equal[:, :], zeros[:, :], 0.0, ALU.add, ALU.add))
                dve.wait_ge(sum_p, BISECTIONS + 1)
                dve.tensor_scalar(need[:, :], SUM[:, 0:1], -1.0, float(CAP), ALU.mult, ALU.add)
                dve.tensor_copy(count[:, :], scan[:, GT - 1:GT]).then_inc(count_d, 1)
                dve.wait_ge(sum_p, BISECTIONS + 2)
                link(dve.tensor_copy(offset[:, 0:1], SUM[:, 0:1]))
                link(dve.tensor_scalar(ties[:, :], scan[:, :], offset[:, 0:1], need[:, :], ALU.add, ALU.is_le))
                link(dve.tensor_tensor(ties[:, :], ties[:, :], equal[:, :], ALU.mult))
                link(dve.tensor_tensor(kept[:, :], ties[:, :], above[:, :], ALU.add))
                link(dve.tensor_tensor_scan(scan[:, :], kept[:, :], zeros[:, :], 0.0, ALU.add, ALU.add))
                dve.tensor_copy(count[:, :], scan[:, GT - 1:GT]).then_inc(count_d, 1)
                dve.wait_ge(sum_p, BISECTIONS + 3)
                link(dve.tensor_copy(offset[:, 1:2], SUM[:, 0:1]))
                link(dve.tensor_scalar(scan[:, :], scan[:, :], offset[:, 1:2], FAR - 1, ALU.add, ALU.add))
                link(dve.scalar_tensor_tensor(place[:, :], kept[:, :], -FAR, scan[:, :], ALU.mult, ALU.add))
                assert done[0] == PLACED, done[0]
                dve.wait_ge(place_p, 1)
                link(dve.tensor_copy(place_t[:, :], PLACE[:, 0:GT]))
                dve.tensor_scalar(parts[:, 0, :], place_t[:, :], SLOT_LO.bit_length() - 1, None, ALU.logical_shift_right)
                link(dve.tensor_scalar(parts[:, 1, :], place_t[:, :], SLOT_LO - 1, None, ALU.bitwise_and))
                dve.tensor_copy(hi[:, :], parts[:, 0, :])
                link(dve.tensor_copy(lo[:, :], parts[:, 1, :]))
                dve.wait_ge(consts, 1)
                for c in range(SLOT_HI):
                    dve.tensor_scalar(is_hi[:, c, :], hi[:, :], float(c), None, ALU.is_equal)
                tokens = token[:, :, :, :].rearrange("p j e t -> p (j e t)")
                for c in range(SLOT_LO):
                    last = dve.scalar_tensor_tensor(lo_token[:, c, :], lo[:, :], float(c), tokens, ALU.is_equal, ALU.mult)
                last.then_inc(onehot_d, 1)
                dve.wait_ge(list_p, 1)
                dve.tensor_scalar(listed[:, :], LIST[0:SLOT_HI, 0:E * SLOT_LO], float(N // 2), None, ALU.add).then_inc(placed, 1)
                dve.wait_ge(placed, 1)



def experts(nc, k, name, rows, lists, w1t, w2t, total):
    SUB = CAP // P
    with ExitStack() as ctx:
        def sb(n, shape, dt=fp32):
            return ctx.enter_context(nc.sbuf_tensor(f"{name}_{n}", shape, dt))

        def sem(n):
            return nc.alloc_semaphore(f"{name}_{n}")

        RING = 3
        assert (E - 2) % RING == 0
        index = sb("index", [P, E, SUB], u32)
        rowsb = sb("rows", [P, RING, SUB, ROW])
        w1 = sb("w1", [P, RING, C, F])
        w2 = sb("w2", [P, RING, FC, D])
        xT = sb("xT", [P, RING, C, CAP])
        hid = sb("hid", [P, RING, FC, CAP])
        y = sb("y", [P, RING, SUB, D])
        index_l, scatter_s, xT_p, xT_d, up_p, hid_d, down_p, y_d = (sem(n) for n in (
            "index_l", "scatter_s", "xT_p", "xT_d", "up_p", "hid_d", "down_p", "y_d"))
        gather_l = [sem(f"gather_l{q}") for q in range(RING)]
        w_l = [sem(f"w_l{q}") for q in range(RING)]
        XB, UB, DB = k.bank[0:2], k.bank[2:4], k.bank[4:6]

        def over(eng, body):
            for e in range(2):
                body(e, e, 0)
            with eng.Fori(0, (E - 2) // RING) as n:
                for u in range(RING):
                    body(n * RING + (2 + u), (2 + u) % RING, n + (2 + u) // RING)

        with nc.Block() as block:
            @block.sync
            def _(sp):
                sp.dma_start(index[:, :, :], lists.rearrange("e (p s) -> p e s", p=P).bitcast(u32)).then_inc(index_l, 16)

                def body(e, q, turn):
                    if later(e, 2):
                        sp.wait_ge(down_p, (e - 1) * 2)
                    sp.dma_start(w1[:, q, :, :], w1t[bass.ds(e * D, D), :].rearrange("(c p) f -> p c f", p=P)).then_inc(w_l[q], 16)
                    sp.dma_start(w2[:, q, :, :], w2t[bass.ds(e * F, F), :].rearrange("(c p) d -> p c d", p=P)).then_inc(w_l[q], 16)
                over(sp, body)
                sp.wait_ge(scatter_s, E * SUB * 16)

            @block.gpsimd
            def _(pool):
                def gather(e):
                    for s in range(SUB):
                        pool.indirect_dma_start(
                            out=rowsb[:, e % RING, s, :], out_offset=None, in_=rows,
                            in_offset=bass.IndirectOffsetOnAxis(ap=index[:, e, s:s + 1], axis=0),
                            compute_op=ALU.bypass).then_inc(gather_l[e % RING], 16)

                def scatter(e, q):
                    pool.wait_ge(y_d, (e + 1) * 2)
                    if later(e, 1):
                        pool.wait_ge(scatter_s, e * SUB * 16)
                    for s in range(SUB):
                        pool.indirect_dma_start(
                            out=total, out_offset=bass.IndirectOffsetOnAxis(ap=index[:, e, s:s + 1], axis=0),
                            in_=y[:, q, s, :], in_offset=None,
                            compute_op=ALU.add).then_inc(scatter_s, 16)

                pool.wait_ge(index_l, 16)
                for e in range(RING):
                    gather(e)
                for e in range(E):
                    scatter(e, e % RING)
                    if e + RING < E:
                        gather(e + RING)

            @block.scalar
            def _(act):
                def body(e, q, turn):
                    for c in range(C):
                        act.wait_ge(xT_p, e * C + (c + 1))
                        if later(e, 2):
                            act.wait_ge(up_p, (e - 1) * FC)
                        act.activation(xT[:, q, c, :], XB[c][:, :], ACT.Copy).then_inc(xT_d, 1)
                    for f in range(FC):
                        act.wait_ge(up_p, e * FC + (f + 1))
                        if later(e, 2):
                            act.wait_ge(down_p, (e - 1) * 2)
                        act.activation(hid[:, q, f, :], UB[f][:, :], ACT.Gelu).then_inc(hid_d, 1)
                over(act, body)

            @block.vector
            def _(dve):
                def body(e, q, turn):
                    for half in range(2):
                        dve.wait_ge(down_p, e * 2 + (half + 1))
                        if later(e, 2):
                            dve.wait_ge(scatter_s, (e - 1) * SUB * 16)
                        for s in range(2 * half, 2 * half + 2):
                            last = dve.tensor_scalar(y[:, q, s, :], DB[half][:, (s % 2) * D:(s % 2 + 1) * D],
                                                     rowsb[:, q, s, bass.ds(D + e, 1)], None, ALU.mult)
                        last.then_inc(y_d, 1)
                over(dve, body)

            @block.tensor
            def _(pe):
                def body(e, q, turn):
                    pe.wait_ge(gather_l[q], (turn + 1) * SUB * 16)
                    for c in range(C):
                        if later(e, 1):
                            pe.wait_ge(xT_d, (e - 1) * C + (c + 1))
                        for s in range(SUB):
                            last = pe.transpose(XB[c][:, s * P:(s + 1) * P], rowsb[:, q, s, c * P:(c + 1) * P], k.ident[:, :])
                        last.then_inc(xT_p, 1)
                    pe.wait_ge(w_l[q], (turn + 1) * 32)
                    pe.wait_ge(xT_d, (e + 1) * C)
                    for f in range(FC):
                        if later(e, 1):
                            pe.wait_ge(hid_d, (e - 1) * FC + (f + 1))
                        for c in range(C):
                            last = pe.matmul(UB[f][:, :], w1[:, q, c, f * P:(f + 1) * P], xT[:, q, c, :],
                                             start=(c == 0), stop=(c == C - 1))
                        last.then_inc(up_p, 1)
                    pe.wait_ge(hid_d, (e + 1) * FC)
                    for half in range(2):
                        if later(e, 1):
                            pe.wait_ge(y_d, (e - 1) * 2 + (half + 1))
                        for s in range(2 * half, 2 * half + 2):
                            for f in range(FC):
                                last = pe.matmul(DB[half][:, (s % 2) * D:(s % 2 + 1) * D], hid[:, q, f, s * P:(s + 1) * P],
                                                 w2[:, q, f, :], start=(f == 0), stop=(f == FC - 1))
                        last.then_inc(down_p, 1)
                over(pe, body)



def windowed_attention(nc, k, x_in, wqk, bqk, w_gate, b_gate, w_proj, b_proj, x_base, rows):
    SCALE = float(HD) ** -0.5
    TOP = 2.0 ** 14
    with ExitStack() as ctx:
        def sb(name, shape, dt=fp32):
            return ctx.enter_context(nc.sbuf_tensor("wa_" + name, shape, dt))

        def sem(name):
            return nc.alloc_semaphore("wa_" + name)

        w = sb("w", [P, C, 2 * D])
        w_g = sb("w_g", [P, C, H])
        w_p = sb("w_p", [P, C, D])
        b_qk = sb("b_qk", [P, 2 * D])
        b_g = sb("b_g", [P, H])
        b_p = sb("b_p", [P, D])
        mask_q, mask_k, tied_q, tied_k = k.mask_q, k.mask_k, k.tied_q, k.tied_k
        pen = sb("pen", [P, 2, TILES])
        penalty = sb("penalty", [P, 2, 2])
        stats, mv, veps, rstd = (sb(n, [P, 2, 6]) for n in ("stats", "mv", "veps", "rstd"))
        stats2, mv2, veps2, rstd2 = (sb(n, [P, 2, 6]) for n in ("stats2", "mv2", "veps2", "rstd2"))
        xn = sb("xn", [P, 2, D])
        xT = sb("xT", [P, 2, C, P])
        qk = sb("qk", [P, 2, 2 * D])
        gl, gm, gex, gsum, ginv = (sb(n, [P, 4, H]) for n in ("gl", "gm", "gex", "gsum", "ginv"))
        v1 = sb("v1", [P, 4, H, 2 * HD])
        stack = sb("stack", [P, 2, 2, H, 4, HD], fp16)
        qS = sb("qS", [P, 2, H // 2, P], fp16)
        qM = sb("qM", [P, 2, H // 2, P], fp16)
        kS = sb("kS", [P, 4, H // 2, P], fp16)
        mdiag = sb("mdiag", [P, H])
        mtied = sb("mtied", [P, H])
        mfar = sb("mfar", [P, 2])
        mall = sb("mall", [P, 2, H])
        pd = sb("pd", [P, 4, 4, P])
        pt = sb("pt", [P, TIED_ALL])
        outT = sb("outT", [P, 2, 4, P])
        rden = sb("rden", [P, 2, H])
        gate = sb("gate", [P, 2, H])
        o = sb("o", [P, 2, H, HD])
        oT = sb("oT", [P, 2, C, P])
        xb = sb("xb", [P, 2, D])
        x1 = sb("x1", [P, 2, D])
        xn2 = sb("xn2", [P, 2, D])
        x2T = sb("x2T", [P, 2, C, P])

        NAMES = ("w_loaded", "x_first", "x_loaded", "fill", "dfill", "consts", "stats_d", "mv_d", "veps_d", "rstd_d", "xn_d",
                 "xT_p", "xT_d", "qk_p", "gl_p", "qk_d", "gl_d", "gm_d", "gn_d", "gex_d", "ginv_d", "v_d", "hi_d", "lo_d",
                 "qS_p", "kS_p", "qS_d", "kS_d", "m_p", "red_d", "mall_d", "mhead_d", "mneg_d", "mS_p", "mS_d", "t_p", "exp_d",
                 "out_p", "outT_d", "o2_p", "rden_d", "gate_d", "o_d", "oT_p", "oT_d", "y_p", "xb_d", "x1_d", "stats2_d",
                 "mv2_d", "veps2_d", "rstd2_d", "xn2_d", "x2T_p", "x2T_d", "lg_p", "lg_d", "x1_s", "xn2_s")
        (w_loaded, x_first, x_loaded, fill, dfill, consts, stats_d, mv_d, veps_d, rstd_d, xn_d,
         xT_p, xT_d, qk_p, gl_p, qk_d, gl_d, gm_d, gn_d, gex_d, ginv_d, v_d, hi_d, lo_d,
         qS_p, kS_p, qS_d, kS_d, m_p, red_d, mall_d, mhead_d, mneg_d, mS_p, mS_d, t_p, exp_d,
         out_p, outT_d, o2_p, rden_d, gate_d, o_d, oT_p, oT_d, y_p, xb_d, x1_d, stats2_d,
         mv2_d, veps2_d, rstd2_d, xn2_d, x2T_p, x2T_d, lg_p, lg_d, x1_s, xn2_s) = (sem(n) for n in NAMES)
        X, QK, T1, M0, M1, P0, P1, O = k.bank
        MB, PB = [M0, M1], [P0, P1]
        XCHUNK = 4
        LO, HI, LAST = 5, 29, TILES + 2

        def at_tile(t):
            return k.x[:, bass.ds(t, 1), :].squeeze(1)

        with nc.Block() as block:
            @block.sync
            def _(sp):
                x_view = x_in.rearrange("(t p) d -> p t d", p=P)
                for g in range(TILES // XCHUNK):
                    sp.dma_start(k.x[:, g * XCHUNK:(g + 1) * XCHUNK, :],
                                 x_view[:, g * XCHUNK:(g + 1) * XCHUNK, :]).then_inc(x_first if g == 0 else x_loaded, 16)
                    if g == 0:
                        sp.dma_start(w[:, :, :], wqk.rearrange("(c p) n -> p c n", p=P)).then_inc(w_loaded, 16)
                        sp.dma_start(w_g[:, :, :], w_gate.rearrange("(c p) n -> p c n", p=P)).then_inc(w_loaded, 16)
                        sp.dma_start(w_p[:, :, :], w_proj.rearrange("(c p) n -> p c n", p=P)).then_inc(w_loaded, 16)
                        for dst, src in ((b_qk, bqk), (b_g, b_gate), (b_p, b_proj)):
                            sp.dma_start(dst[:, :], src.partition_broadcast(P)).then_inc(w_loaded, 16)

                def slot(i, p):
                    t = i - 2
                    if active(t):
                        sp.wait_ge(x1_d, t + 1)
                        sp.dma_start(x_base[bass.ds(t * P, P), :], x1[:, p % 2, :]).then_inc(x1_s, 16)
                        sp.wait_ge(xn2_d, t + 1)
                        sp.dma_start(rows[bass.ds(t * P, P), 0:D], xn2[:, p % 2, :]).then_inc(xn2_s, 16)
                pipeline(sp, slot, 2, LO, HI, LAST, 4)
                sp.wait_ge(w_loaded, 6 * 16)
                sp.wait_ge(x1_s, 16 * TILES)
                sp.wait_ge(xn2_s, 16 * TILES)

            @block.gpsimd
            def _(pool):
                pool.wait_ge(w_loaded, 6 * 16)

                def slot(i, p):
                    t, q = i + 2, p % 2
                    if active(t):
                        pool.wait_ge(mv_d, t + 1)
                        pool.tensor_tensor(veps[:, q, 0:1], mv[:, q, 1:2], k.eps[:, :], ALU.add).then_inc(veps_d, 1)
                        pool.wait_ge(veps_d, t + 1)
                        pool.tensor_tensor(rstd[:, q, 0:1], veps[:, q, 0:1], k.half[:, :], ALU.pow).then_inc(rstd_d, 1)
                    t, q = i, p % 2
                    if active(t):
                        pool.wait_ge(xn_d, t + 1)
                        if later(t, 2):
                            pool.wait_ge(x1_d, t - 1)
                        pool.tensor_tensor(xb[:, q, :], at_tile(t), b_p[:, :], ALU.add).then_inc(xb_d, 1)
                    t, q = i - 2, p % 2
                    if active(t):
                        pool.wait_ge(mv2_d, t + 1)
                        pool.tensor_tensor(veps2[:, q, 0:1], mv2[:, q, 1:2], k.eps[:, :], ALU.add).then_inc(veps2_d, 1)
                        pool.wait_ge(veps2_d, t + 1)
                        pool.tensor_tensor(rstd2[:, q, 0:1], veps2[:, q, 0:1], k.half[:, :], ALU.pow).then_inc(rstd2_d, 1)
                pipeline(pool, slot, -2, LO, HI, LAST, 4)

            @block.vector
            def _(dve):
                dve.memset(v1[:, :, :, :], 1.0).then_inc(dfill, 1)
                dve.memset(stack[:, :, :, :, :, :], 0.0).then_inc(dfill, 1)
                dve.memset(kS[:, :, :, :], 0.0).then_inc(dfill, 1)
                dve.memset(pen[:, :, :], 0.0).then_inc(dfill, 1)
                dve.wait_ge(dfill, 4)
                dve.memset(stack[:, :, 1, :, 3, 0], TOP).then_inc(dfill, 1)
                for b in range(B):
                    dve.memset(pen[:, 0, b * SEQ_TILES:b * SEQ_TILES + 1], -BIG).then_inc(dfill, 1)
                    dve.memset(pen[:, 1, b * SEQ_TILES:b * SEQ_TILES + 2], -BIG).then_inc(dfill, 1)
                dve.wait_ge(dfill, 9)
                dve.memset(gsum[:, :, :], 0.0).then_inc(consts, 1)
                dve.wait_ge(w_loaded, 6 * 16)

                def maxima(t, g):
                    dve.wait_ge(m_p, t * 6 + (g + 1))
                    bank = MB[g % 2]
                    if g < 4:
                        dve.reduce_max(mdiag[:, 4 * g:4 * g + 4], bank[:, :].rearrange("p (h s) -> p h s", s=P),
                                       AX.X).then_inc(red_d, 1)
                        return
                    strips = [s for s in TIED[g - 4][0] if s[0] < 8]
                    for h, back, n, at in strips:
                        dst = mtied[:, place_of(h):place_of(h) + 1] if back == 1 else mfar[:, 0:1]
                        dve.reduce_max(dst, bank[:, at:at + n], AX.X)
                    at = [s[3] for s in TIED[g - 4][0] if s[0] >= 8][0]
                    n = REACH[H - 1]
                    first = place_of(8 + g - 4)
                    dve.reduce_max(mtied[:, first:first + 4], bank[:, at:at + 4 * n].rearrange("p (h s) -> p h s", s=n),
                                   AX.X).then_inc(red_d, 1)

                def slot(i, p):
                    t = i
                    if active(t):
                        if later(t, 1):
                            dve.wait_ge(mneg_d, t)
                        maxima(t, 0)
                        maxima(t, 1)
                    t, q = i - 3, (p + 1) % 2
                    if active(t):
                        dve.wait_ge(rstd2_d, t + 1)
                        dve.wait_ge(mv2_d, t + 1)
                        if later(t, 2):
                            dve.wait_ge(x2T_p, t - 1)
                        if later(t, 1):
                            dve.wait_ge(xn2_s, t * 16)
                        dve.tensor_scalar(xn2[:, q, :], x1[:, q, :], mv2[:, q, 0:1], rstd2[:, q, 0:1],
                                          ALU.subtract, ALU.mult).then_inc(xn2_d, 1)
                    t, q = i - 2, p % 2
                    if active(t):
                        o2 = T1[:, :].rearrange("p (h c) -> p h c", h=H)
                        dve.wait_ge(o2_p, t + 1)
                        dve.reciprocal(rden[:, q, :], o2[:, :, HD]).then_inc(rden_d, 1)
                        dve.wait_ge(rden_d, t + 1)
                        dve.scalar_tensor_tensor(gate[:, q, :], gex[:, (p - 2) % 4, :], ginv[:, (p - 2) % 4, 0:1], rden[:, q, :],
                                                 ALU.mult, ALU.mult).then_inc(gate_d, 1)
                        dve.wait_ge(gate_d, t + 1)
                        dve.tensor_tensor(o[:, q, :, :], o2[:, :, 0:HD],
                                          gate[:, q, :].unsqueeze(2).broadcast_to([P, H, HD]), ALU.mult).then_inc(o_d, 1)
                    t, q = i, p % 2
                    if active(t):
                        dve.tensor_copy(penalty[:, q, :], pen[:, :, bass.ds(t, 1)].squeeze(2))
                        maxima(t, 2)
                    t, q = i + 2, p % 2
                    if active(t):
                        dve.wait_ge(x_first, 16)
                        if later(t, XCHUNK):
                            dve.wait_ge(x_loaded, 16 * (TILES // XCHUNK - 1))
                        dve.bn_stats(stats[:, q, 0:6], at_tile(t)).then_inc(stats_d, 1)
                        dve.wait_ge(stats_d, t + 1)
                    t = i
                    if active(t):
                        maxima(t, 3)
                    t, q = i + 2, p % 2
                    if active(t):
                        dve.bn_aggr(mv[:, q, 0:2], stats[:, q, 0:6]).then_inc(mv_d, 1)
                    t, q, r = i + 1, (p + 1) % 2, (p + 1) % 4
                    if active(t):
                        dve.wait_ge(qk_p, t + 1)
                        dve.tensor_tensor(qk[:, q, :], QK[:, :], b_qk[:, :], ALU.add).then_inc(qk_d, 1)
                        dve.wait_ge(gl_p, t + 1)
                        dve.tensor_tensor(gl[:, r, :], X[:, 0:H], b_g[:, :], ALU.add).then_inc(gl_d, 1)
                        dve.wait_ge(gl_d, t + 1)
                        dve.reduce_max(gm[:, r, 0:1], gl[:, r, :], AX.X).then_inc(gm_d, 1)
                        dve.wait_ge(gm_d, t + 1)
                        dve.tensor_scalar(gm[:, r, 1:2], gm[:, r, 0:1], -1.0, None, ALU.mult).then_inc(gn_d, 1)
                        dve.wait_ge(qk_d, t + 1)
                        if later(t, 2):
                            dve.wait_ge(kS_p, t - 1)
                            dve.wait_ge(mS_p, t - 1)
                        qv = qk[:, q, :].rearrange("p (n h d) -> p n h d", n=2, h=H)
                        dve.tensor_copy(stack[:, q, 0, :, 0:2, :],
                                        qv[:, 0, :, :].unsqueeze(2).broadcast_to([P, H, 2, HD])).then_inc(hi_d, 1)
                        dve.tensor_copy(stack[:, q, 1, :, 0:3:2, :],
                                        qv[:, 1, :, :].unsqueeze(2).broadcast_to([P, H, 2, HD])).then_inc(hi_d, 1)
                        dve.memset(stack[:, q, 0, :, 3, 0], 0.0).then_inc(hi_d, 1)
                        dve.wait_ge(hi_d, (t + 1) * 3)
                        dve.tensor_tensor(stack[:, q, 0, :, 2, :], qv[:, 0, :, :], stack[:, q, 0, :, 0, :],
                                          ALU.subtract).then_inc(lo_d, 1)
                        dve.tensor_tensor(stack[:, q, 1, :, 1, :], qv[:, 1, :, :], stack[:, q, 1, :, 0, :],
                                          ALU.subtract).then_inc(lo_d, 1)
                    t, q = i, p % 2
                    if active(t):
                        maxima(t, 4)
                        maxima(t, 5)
                        dve.wait_ge(red_d, (t + 1) * 6)
                        dve.scalar_tensor_tensor(mall[:, q, :], mtied[:, :], pen[:, 0, bass.ds(t, 1)], mdiag[:, :],
                                                 ALU.add, ALU.max).then_inc(mall_d, 1)
                    t, q = i - 2, p % 2
                    if active(t):
                        dve.wait_ge(y_p, t + 1)
                        dve.wait_ge(xb_d, t + 1)
                        if later(t, 1):
                            dve.wait_ge(x1_s, t * 16)
                        dve.tensor_tensor(x1[:, q, :], T1[:, 0:D], xb[:, q, :], ALU.add).then_inc(x1_d, 1)
                    t, q = i, p % 2
                    if active(t):
                        dve.wait_ge(mall_d, t + 1)
                        dve.scalar_tensor_tensor(mall[:, q, 0:1], mfar[:, 0:1], pen[:, 1, bass.ds(t, 1)], mall[:, q, 0:1],
                                                 ALU.add, ALU.max).then_inc(mhead_d, 1)
                    t, q = i - 2, p % 2
                    if active(t):
                        dve.wait_ge(x1_d, t + 1)
                        dve.bn_stats(stats2[:, q, 0:6], x1[:, q, :]).then_inc(stats2_d, 1)
                        dve.wait_ge(stats2_d, t + 1)
                    t, q = i, p % 2
                    if active(t):
                        dve.wait_ge(mhead_d, t + 1)
                        dve.wait_ge(qS_p, t + 1)
                        dve.tensor_scalar(stack[:, q, 0, :, 3, 0].rearrange("p (a j b) -> p a b j", a=2, b=2),
                                          mall[:, q, :].rearrange("p (a b j) -> p a b j", a=2, b=2), -1.0 / TOP, None,
                                          ALU.mult).then_inc(mneg_d, 1)
                    t, r = i + 1, (p + 1) % 4
                    if active(t):
                        dve.wait_ge(kS_p, t + 1)
                        dve.tensor_copy(kS[:, r, :, :], QK[:, :].bitcast(fp16).rearrange("p (h t) -> p h t", t=P)).then_inc(kS_d, 1)
                        dve.wait_ge(gex_d, t + 1)
                        dve.reciprocal(ginv[:, r, 0:1], gsum[:, r, 0:1]).then_inc(ginv_d, 1)
                    t, q = i - 2, p % 2
                    if active(t):
                        dve.bn_aggr(mv2[:, q, 0:2], stats2[:, q, 0:6]).then_inc(mv2_d, 1)
                    t, q = i + 2, p % 2
                    if active(t):
                        dve.wait_ge(rstd_d, t + 1)
                        dve.wait_ge(mv_d, t + 1)
                        if later(t, 2):
                            dve.wait_ge(xT_p, t - 1)
                        dve.tensor_scalar(xn[:, q, :], at_tile(t), mv[:, q, 0:1], rstd[:, q, 0:1],
                                          ALU.subtract, ALU.mult).then_inc(xn_d, 1)
                pipeline(dve, slot, -2, LO, HI, LAST, 4)

            @block.scalar
            def _(act):
                act.wait_ge(consts, 1)

                def expo(t, par, n, g):
                    act.wait_ge(t_p, t * 6 + (n + 1))
                    if n < 2:
                        width = TIED[n][1]
                        if n == 0:
                            act.activation(pt[:, 0:P], PB[0][:, 0:P], ACT.Exp, bias=penalty[:, par, 1:2], scale=SCALE)
                        at = P if n == 0 else 0
                        act.activation(pt[:, TIED_AT[n] + at:TIED_AT[n] + width], PB[n][:, at:width], ACT.Exp,
                                       bias=penalty[:, par, 0:1], scale=SCALE).then_inc(exp_d, 1)
                    else:
                        act.activation(pd[:, g, :, :], PB[n % 2][:, :].rearrange("p (h t) -> p h t", t=P), ACT.Exp,
                                       scale=SCALE).then_inc(exp_d, 1)

                def slot(i, p):
                    t, q = i + 1, (p + 1) % 2
                    if active(t):
                        act.wait_ge(xT_p, t + 1)
                        if later(t, 2):
                            act.wait_ge(gl_p, t - 1)
                        act.activation(xT[:, q, :, :], X[:, 0:D].rearrange("p (c t) -> p c t", c=C), ACT.Copy).then_inc(xT_d, 1)
                    t = i - 1
                    if active(t):
                        if later(t, 1):
                            act.wait_ge(out_p, t)
                        expo(t, (p + 1) % 2, 0, 0)
                        expo(t, (p + 1) % 2, 1, 0)
                        expo(t, (p + 1) % 2, 2, 0)
                        expo(t, (p + 1) % 2, 3, 1)
                    t, q = i - 2, p % 2
                    if active(t):
                        act.wait_ge(oT_p, t + 1)
                        if later(t, 2):
                            act.wait_ge(y_p, t - 1)
                        act.activation(oT[:, q, :, :], T1[:, 0:D].rearrange("p (c t) -> p c t", c=C), ACT.Copy).then_inc(oT_d, 1)
                    t, r = i + 1, (p + 1) % 4
                    if active(t):
                        act.wait_ge(gn_d, t + 1)
                        act.activation(gex[:, r, :], gl[:, r, :], ACT.Exp, bias=gm[:, r, 1:2],
                                       accum_out=gsum[:, r, 0:1]).then_inc(gex_d, 1)
                    t, q = i - 3, (p + 1) % 2
                    if active(t):
                        act.wait_ge(x2T_p, t + 1)
                        if later(t, 2):
                            act.wait_ge(lg_p, t - 1)
                        act.activation(x2T[:, q, :, :], X[:, 0:D].rearrange("p (c t) -> p c t", c=C), ACT.Copy).then_inc(x2T_d, 1)
                    t = i - 1
                    if active(t):
                        expo(t, (p + 1) % 2, 4, 2)
                        expo(t, (p + 1) % 2, 5, 3)
                    t = i - 3
                    if active(t):
                        act.wait_ge(lg_p, t + 1)
                        act.activation(k.logits[:, bass.ds(t, 1), :].squeeze(1), X[:, 0:E], ACT.Copy).then_inc(lg_d, 1)
                    t, q = i + 1, (p + 1) % 2
                    if active(t):
                        act.wait_ge(qS_p, t + 1)
                        act.activation(qS[:, q, :, :], T1[:, :].bitcast(fp16).rearrange("p (h t) -> p h t", t=P), ACT.Copy).then_inc(qS_d, 1)
                    t, q = i - 1, (p + 1) % 2
                    if active(t):
                        act.wait_ge(out_p, t + 1)
                        if later(t, 2):
                            act.wait_ge(o2_p, t - 1)
                        act.activation(outT[:, q, :, :], O[:, :].rearrange("p (g t) -> p g t", g=4), ACT.Copy).then_inc(outT_d, 1)
                    t, q, r = i + 1, (p + 1) % 2, (p + 1) % 4
                    if active(t):
                        act.wait_ge(qk_d, t + 1)
                        for a in range(2):
                            last = act.activation(
                                v1[:, r, 8 * a:8 * a + 8, 0:HD].rearrange("p (b j) d -> p b j d", b=2),
                                qk[:, q, D + a * P:D + (a + 1) * P].rearrange("p (j b d) -> p b j d", b=2, d=HD), ACT.Copy)
                        last.then_inc(v_d, 1)
                    t, q = i, p % 2
                    if active(t):
                        act.wait_ge(mS_p, t + 1)
                        if later(t, 2):
                            act.wait_ge(t_p, (t - 1) * 6)
                        act.activation(qM[:, q, :, :], T1[:, :].bitcast(fp16).rearrange("p (h t) -> p h t", t=P), ACT.Copy).then_inc(mS_d, 1)
                pipeline(act, slot, -1, LO, HI, LAST, 4)

            @block.tensor
            def _(pe):
                pe.wait_ge(w_loaded, 6 * 16)
                pe.wait_ge(consts, 1)

                def transpose2(bank, src, done):
                    for c in range(C):
                        last = pe.transpose(bank[:, c * P:(c + 1) * P], src[:, c * P:(c + 1) * P], k.ident[:, :])
                    last.then_inc(done, 1)

                def q_stack(t, q, done):
                    for h in range(H // 2):
                        last = pe.transpose(T1[:, :].bitcast(fp16)[:, h * P:(h + 1) * P],
                                            stack[:, q, 0, 2 * h:2 * h + 2, :, :].rearrange("p h n d -> p (h n d)"), k.ident16[:, :])
                    last.then_inc(done, 1)

                def for_max(t, p, n):
                    if n >= 2 or later(t, 1):
                        pe.wait_ge(red_d, t * 6 + (n - 1))
                    q, r = p % 2, 64 * (n % 2)
                    bank = MB[n % 2]
                    if n < 4:
                        pe.matmul(bank[:, :], k.identb[:, :], mask_q[:, n, :, :].rearrange("p h s -> p (h s)"), start=True, stop=True,
                                  skip_group_check=True)
                        for j in range(4):
                            h = head(n, j)
                            last = pe.matmul(bank[:, j * P:(j + 1) * P], qS[r:r + 64, q, h // 2, :],
                                             kS[r:r + 64, p % 4, h // 2, :], start=False, stop=True, skip_group_check=True)
                    else:
                        strips, width = TIED[n - 4]
                        pe.matmul(bank[:, 0:width], k.identb[:, :], tied_q[:, TIED_AT[n - 4]:TIED_AT[n - 4] + width],
                                  start=True, stop=True, skip_group_check=True)
                        for h, back, m, at in strips:
                            last = pe.matmul(bank[:, at:at + m], qS[r:r + 64, q, h // 2, :],
                                             kS[r:r + 64, (p - back) % 4, h // 2, P - m:P], start=False, stop=True,
                                             skip_group_check=True)
                    last.then_inc(m_p, 1)

                def for_exp(t, p, n):
                    if n >= 2 or later(t, 1):
                        pe.wait_ge(exp_d, t * 6 + (n - 1))
                    q, r = p % 2, 64 * (n % 2)
                    bank = PB[n % 2]
                    if n < 2:
                        strips, width = TIED[n]
                        pe.matmul(bank[:, 0:width], k.identb[:, :], tied_k[:, TIED_AT[n]:TIED_AT[n] + width],
                                  start=True, stop=True, skip_group_check=True)
                    else:
                        strips = [(head(n - 2, j), 0, P, j * P) for j in range(4)]
                        pe.matmul(bank[:, :], k.identb[:, :], mask_k[:, n - 2, :, :].rearrange("p h s -> p (h s)"), start=True, stop=True,
                                  skip_group_check=True)
                    for h, back, m, at in strips:
                        last = pe.matmul(bank[:, at:at + m], kS[r:r + 64, (p - back) % 4, h // 2, :],
                                         qM[r:r + 64, q, h // 2, 0:m], start=False, stop=True, skip_group_check=True)
                    last.then_inc(t_p, 1)

                def attend(t, p, n):
                    pe.wait_ge(exp_d, t * 6 + (n + 1))
                    if n < 2:
                        todo = [(h, back, m, pt[:, TIED_AT[n] + at:TIED_AT[n] + at + m]) for h, back, m, at in TIED[n][0]]
                    else:
                        todo = [(head(n - 2, j), 0, P, pd[:, n - 2, j, :]) for j in range(4)]
                    for h, back, m, src in todo:
                        g, j = divmod(place_of(h), 4)
                        last = pe.matmul(O[32 * j:32 * j + 32, g * P:g * P + m], v1[:, (p - back) % 4, place_of(h), :], src,
                                         start=(n == 2), stop=True, skip_group_check=True)
                    return last

                def slot(i, p):
                    t, q = i + 1, (p + 1) % 2
                    if active(t):
                        pe.wait_ge(xn_d, t + 1)
                        if later(t, 5):
                            pe.wait_ge(lg_d, t - 4)
                        elif t > 0:
                            pe.wait_ge(gl_d, t)
                        transpose2(X, xn[:, q, :], xT_p)
                    t = i
                    if active(t):
                        pe.wait_ge(qS_d, t + 1)
                        pe.wait_ge(kS_d, t + 1)
                        for_max(t, p, 0)
                        for_max(t, p, 1)
                    t = i - 1
                    if active(t):
                        pe.wait_ge(mS_d, t + 1)
                        for_exp(t, p - 1, 0)
                        for_exp(t, p - 1, 1)
                    t, q = i - 2, p % 2
                    if active(t):
                        pe.wait_ge(outT_d, t + 1)
                        if active(i - 1):
                            pe.wait_ge(mS_d, t + 2)
                        else:
                            pe.wait_ge(x1_d, t)
                        for g in range(4):
                            last = pe.transpose(T1[:, g * P:(g + 1) * P], outT[:, q, g, :], k.ident[:, :])
                        last.then_inc(o2_p, 1)
                    t, q = i + 1, (p + 1) % 2
                    if active(t):
                        pe.wait_ge(xT_d, t + 1)
                        if later(t, 1):
                            pe.wait_ge(kS_d, t)
                        for c in range(C):
                            last = pe.matmul(QK[:, :], xT[:, q, c, :], w[:, c, :], start=(c == 0), stop=(c == C - 1))
                        last.then_inc(qk_p, 1)
                        for c in range(C):
                            last = pe.matmul(X[:, 0:H], xT[:, q, c, :], w_g[:, c, :], start=(c == 0), stop=(c == C - 1))
                        last.then_inc(gl_p, 1)
                    t = i
                    if active(t):
                        for_max(t, p, 2)
                        for_max(t, p, 3)
                    t = i - 1
                    if active(t):
                        for_exp(t, p - 1, 2)
                        for_exp(t, p - 1, 3)
                    t, q = i - 2, p % 2
                    if active(t):
                        pe.wait_ge(o_d, t + 1)
                        transpose2(T1, o[:, q, :, :].rearrange("p h d -> p (h d)"), oT_p)
                    t = i - 1
                    if active(t):
                        pe.wait_ge(v_d, t + 1)
                        if later(t, 1):
                            pe.wait_ge(outT_d, t)
                        attend(t, p - 1, 2)
                        attend(t, p - 1, 3)
                    t, q = i - 3, (p + 1) % 2
                    if active(t):
                        pe.wait_ge(xn2_d, t + 1)
                        if active(i + 1):
                            pe.wait_ge(gl_d, t + 5)
                        else:
                            pe.wait_ge(lg_d, t)
                        transpose2(X, xn2[:, q, :], x2T_p)
                    t = i
                    if active(t):
                        for_max(t, p, 4)
                        for_max(t, p, 5)
                    t, q = i - 2, p % 2
                    if active(t):
                        pe.wait_ge(oT_d, t + 1)
                        for c in range(C):
                            last = pe.matmul(T1[:, 0:D], oT[:, q, c, :], w_p[:, c, :], start=(c == 0), stop=(c == C - 1))
                        last.then_inc(y_p, 1)
                    t = i - 1
                    if active(t):
                        for_exp(t, p - 1, 4)
                        for_exp(t, p - 1, 5)
                    t, q = i - 3, (p + 1) % 2
                    if active(t):
                        pe.wait_ge(x2T_d, t + 1)
                        for c in range(C):
                            last = pe.matmul(X[:, 0:E], x2T[:, q, c, :], k.wg[:, c, :], start=(c == 0), stop=(c == C - 1))
                        last.then_inc(lg_p, 1)
                    t = i - 1
                    if active(t):
                        attend(t, p - 1, 0)
                        attend(t, p - 1, 1)
                    t, q = i + 1, (p + 1) % 2
                    if active(t):
                        pe.wait_ge(lo_d, (t + 1) * 2)
                        if later(t, 3):
                            pe.wait_ge(x1_d, t - 2)
                        elif t == 2:
                            pe.wait_ge(mS_d, 1)
                        elif t == 1:
                            pe.wait_ge(qS_d, 1)
                        q_stack(t, q, qS_p)
                        for h in range(H // 2):
                            last = pe.transpose(QK[:, :].bitcast(fp16)[:, h * P:(h + 1) * P],
                                                stack[:, q, 1, 2 * h:2 * h + 2, :, :].rearrange("p h n d -> p (h n d)"), k.ident16[:, :])
                        last.then_inc(kS_p, 1)
                    t = i - 1
                    if active(t):
                        attend(t, p - 1, 4)
                        attend(t, p - 1, 5).then_inc(out_p, 1)
                    t, q = i, p % 2
                    if active(t):
                        pe.wait_ge(mneg_d, t + 1)
                        if active(i + 1):
                            pe.wait_ge(qS_d, t + 2)
                        else:
                            pe.wait_ge(x1_d, t - 1)
                        q_stack(t, q, mS_p)
                pipeline(pe, slot, -1, LO, HI, LAST, 4)



def hybrid_block(nc, x, wq, wk, wv, wo, wqk, bqk, w_gate, b_gate, w_proj, b_proj, gate_wt, w1t, w2t, out):
    def scratch(name, shape, dt):
        return nc.dram_tensor(name, shape, dt, kind="Internal").ap()

    middle = scratch("middle", [N, D], fp32)
    with ExitStack() as ctx:
        k = Core(nc, ctx)
        rows, lists = scratch("rows_a", [N, ROW], fp32), scratch("lists_a", [E, CAP], i32)
        with nc.cleanup_on_exit():
            setup(nc, k, gate_wt)
            linear_attention(nc, k, x, wq, wk, wv, wo, middle, rows)
        with nc.cleanup_on_exit():
            router(nc, k, "ra", rows, lists, masks=True)
            experts(nc, k, "fa", rows, lists, w1t, w2t, middle)
        rows, lists = scratch("rows_b", [N, ROW], fp32), scratch("lists_b", [E, CAP], i32)
        with nc.cleanup_on_exit():
            windowed_attention(nc, k, middle, wqk, bqk, w_gate, b_gate, w_proj, b_proj, out, rows)
        with nc.cleanup_on_exit():
            router(nc, k, "rb", rows, lists, masks=False)
            experts(nc, k, "fb", rows, lists, w1t, w2t, out)


def kernel(**inputs):
    import numpy as np
    import concourse.bacc as bacc
    from concourse.bass_utils import run_bass_kernel_spmd

    a = {n: np.asarray(v) for n, v in inputs.items()}

    def by_place(w):
        return w.reshape(2, 4, 2, HD, -1).transpose(0, 2, 1, 3, 4).reshape(w.shape)

    places = np.arange(H).reshape(2, 4, 2).transpose(0, 2, 1).reshape(-1)
    b = {
        "x": a["L0_attn_a_x"].reshape(N, D),
        "wq": a["L0_attn_a_wq"],
        "wk": a["L0_attn_a_wk"],
        "wv": by_place(a["L0_attn_a_wv"].T).T,
        "wo": by_place(a["L0_attn_a_wo"]),
        "wqk": a["L0_attn_b_Wqk"],
        "bqk": a["L0_attn_b_bqk"],
        "w_gate": a["L0_attn_b_Wgate"][:, places],
        "b_gate": a["L0_attn_b_bgate"][places],
        "w_proj": by_place(a["L0_attn_b_Wproj"]),
        "b_proj": a["L0_attn_b_bproj"],
        "gate_wt": a["L0_ffn_gate_w"].T,
        "w1t": a["L0_ffn_w1"].transpose(0, 2, 1).reshape(E * D, F),
        "w2t": a["L0_ffn_w2"].transpose(0, 2, 1).reshape(E * F, D),
    }
    nc = bacc.Bacc("TRN2", target_bir_lowering=False, num_devices=1)
    arrays, args = {}, []
    for name, value in b.items():
        value = np.ascontiguousarray(value)
        arrays[f"in_{name}_dram"] = value
        args.append(nc.dram_tensor(f"in_{name}_dram", value.shape, mybir.dt.from_np(value.dtype), kind="ExternalInput").ap())
    args.append(nc.dram_tensor("out_dram", [N, D], fp32, kind="ExternalOutput").ap())
    hybrid_block(nc, *args)
    r = run_bass_kernel_spmd(nc, [arrays], core_ids=[0])
    return np.asarray(r.results[0]["out_dram"]).reshape(B, S, D)
```

```python
import concourse.bass as bass
from concourse import mybir
from contextlib import ExitStack

fp32 = mybir.dt.float32
fp16 = mybir.dt.float16
bf16 = mybir.dt.bfloat16
i32 = mybir.dt.int32
u32 = mybir.dt.uint32
ALU = mybir.AluOpType
ACT = mybir.ActivationFunctionType
AX = mybir.AxisListType

P = 128
B, S, D = 2, 2048, 256
N = B * S
TILES = N // P
SEQ_TILES = S // P
C = D // P
H = 16
HD = D // H
E = 8
F = 256
FC = F // P
CAP = N // E
EPS_LN = 1e-5
EPS_DEN = 1e-6
BIG = 1e30
ROW = D + E
WINDOWS = [max(4, 256 // 2 ** h) for h in range(H)]
REACH = [min(P, w) for w in WINDOWS]
REACH_AT = [sum(REACH[:h]) for h in range(H)]
REACH_ALL = sum(REACH)
WS = 16.0
ROUNDS = 14
ROUNDS_UNROLLED = 7
GROUPS = P // E
GT = N // GROUPS
SLOT_HI, SLOT_LO = 32, CAP // 32
AHEAD = 6
PLACED = 65


def later(t, n):
    return not isinstance(t, int) or t >= n


def active(t):
    return not isinstance(t, int) or 0 <= t < TILES


def pipeline(eng, slot, first, lo, hi, last, unroll, ring):
    assert (hi - lo) % unroll == 0 and unroll % ring == 0
    for i in range(first, lo):
        slot(i, i % ring)
    with eng.Fori(0, (hi - lo) // unroll) as n:
        for u in range(unroll):
            slot(n * unroll + (lo + u), (lo + u) % ring)
    for i in range(hi, last + 1):
        slot(i, i % ring)


def head(g, j):
    return 8 * (g // 2) + 2 * j + g % 2


def tied(parity):
    strips, at = [], 0
    for back, h in [(2, 0)] * (parity == 0) + [(1, h) for h in range(parity, H, 2)]:
        strips.append((h, back, REACH[h], at))
        at += REACH[h]
    return strips, at


def place_of(h):
    return 8 * (h // 8) + 4 * (h % 2) + (h % 8) // 2


TIED = [tied(0), tied(1)]
TIED_AT = [0, TIED[0][1]]
TIED_ALL = TIED[0][1] + TIED[1][1]


class Core:

    def __init__(self, nc, ctx):
        self.nc, self.ctx = nc, ctx
        self.x = self.sb("x_sb", [P, TILES, D], fp32)
        self.logits = self.sb("logits_sb", [P, TILES, E], fp32)
        self.bank = [self.ps(f"bank{i}") for i in range(8)]
        self.ident = self.sb("ident", [P, P], fp32)
        self.ident16 = self.sb("ident16", [P, P], fp16)
        self.identb = self.sb("identb", [P, P], bf16)
        self.index = self.sb("index", [P, E, CAP // P], i32)
        self.half = self.sb("half", [P, 1], fp32)
        self.eps = self.sb("eps", [P, 1], fp32)
        self.wg = self.sb("wg", [P, C, E], fp32)
        self.wg16 = self.sb("wg16", [P, 2, C, E], fp16)
        self.w, self.w16 = self.sb("w", [P, C, 2 * D], fp32), self.sb("w16", [P, 2, C, 2 * D], fp16)
        self.w_g, self.w_g16 = self.sb("w_g", [P, C, H], fp32), self.sb("w_g16", [P, 2, C, H], fp16)
        self.w_p, self.w_p16 = self.sb("w_p", [P, C, D], fp32), self.sb("w_p16", [P, 2, C, D], fp16)
        self.b_qk, self.b_g, self.b_p = (self.sb(n, [P, m], fp32) for n, m in (("b_qk", 2 * D), ("b_g", H), ("b_p", D)))
        self.mask_q = self.sb("mask_q", [P, 4, 4, P], bf16)
        self.mask_k = self.sb("mask_k", [P, 4, 4, P], bf16)
        self.tied_q = self.sb("tied_q", [P, TIED_ALL], bf16)
        self.tied_k = self.sb("tied_k", [P, TIED_ALL], bf16)

    def sb(self, name, shape, dt):
        return self.ctx.enter_context(self.nc.sbuf_tensor(name, shape, dt))

    def ps(self, name):
        return self.ctx.enter_context(self.nc.psum_tensor(name, [P, 512], fp32))


def setup(nc, k, gate_wt):
    with ExitStack() as ctx:
        zeroed = nc.alloc_semaphore("zeroed")
        ready = nc.alloc_semaphore("ident_ready")
        copied = nc.alloc_semaphore("ident_copied")
        loaded = nc.alloc_semaphore("wg_loaded")
        with nc.Block() as block:
            @block.sync
            def _(sp):
                sp.dma_start(k.wg[:, :, :], gate_wt.rearrange("(c p) e -> p c e", p=P)).then_inc(loaded, 16)
                sp.wait_ge(loaded, 16)

            @block.gpsimd
            def _(pool):
                pool.memset(k.ident[:, :], 0.0).then_inc(zeroed, 1)
                pool.memset(k.half[:, :], -0.5).then_inc(zeroed, 1)
                pool.memset(k.eps[:, :], EPS_LN).then_inc(zeroed, 1)
                pool.wait_ge(zeroed, 3)
                pool.affine_select(out=k.ident[:, :], in_=k.ident[:, :], compare_op=ALU.not_equal, fill=1.0,
                                   base=0, pattern=[[-1, P]], channel_multiplier=1).then_inc(ready, 1)

            @block.vector
            def _(dve):
                dve.wait_ge(ready, 1)
                dve.tensor_copy(k.ident16[:, :], k.ident[:, :]).then_inc(copied, 1)
                dve.tensor_copy(k.identb[:, :], k.ident[:, :]).then_inc(copied, 1)
                dve.wait_ge(loaded, 16)
                dve.tensor_scalar(k.wg16[:, 0, :, :], k.wg[:, :, :], WS, None, ALU.mult).then_inc(copied, 1)
                dve.wait_ge(copied, 3)
                dve.scalar_tensor_tensor(k.wg16[:, 1, :, :], k.wg[:, :, :], WS, k.wg16[:, 0, :, :], ALU.mult,
                                         ALU.subtract).then_inc(copied, 1)
                dve.wait_ge(copied, 4)


def split_product(pe, out, x, w, all_terms=False):
    terms = [(n, m, c) for n, m in ((0, 0), (0, 1), (1, 0), (1, 1))[:4 if all_terms else 3] for c in range(C)]
    for n, m, c in terms:
        last = pe.matmul(out, x[:, n, c, :], w[:, m, c, :], start=((n, m, c) == terms[0]), stop=((n, m, c) == terms[-1]))
    return last


def window_masks(k, pool, fill):
    for m in (k.mask_q[:, :, :, :], k.mask_k[:, :, :, :], k.tied_q[:, :], k.tied_k[:, :]):
        pool.memset(m, 0.0).then_inc(fill, 1)
    pool.wait_ge(fill, 4)
    done = 4

    def select(m, base, mult, step):
        nonlocal done
        pool.affine_select(out=m, in_=m, compare_op=ALU.is_ge, fill=-BIG, base=base,
                           pattern=[[step, m.shape[-1]]], channel_multiplier=mult).then_inc(fill, 1)
        done += 1
    for g in range(4):
        for j in range(4):
            select(k.mask_q[:, g, j, :], 0, 1, -1)
            select(k.mask_k[:, g, j, :], 0, -1, 1)
    pool.wait_ge(fill, done)
    for g in range(4):
        for j in range(4):
            wd = WINDOWS[head(g, j)]
            if wd < P:
                select(k.mask_q[:, g, j, :], wd - 1, -1, 1)
                select(k.mask_k[:, g, j, :], wd - 1, 1, -1)
    for s in range(2):
        for h, back, n, at in TIED[s][0]:
            a = TIED_AT[s] + at
            select(k.tied_q[:, a:a + n], WINDOWS[h] - 1 - back * P + (P - n), -1, 1)
            select(k.tied_k[:, a:a + n], WINDOWS[h] - 1 - back * P, 1, -1)
    pool.wait_ge(fill, done)



def linear_attention(nc, k, x_in, wq, wk, wv, wo, x_base, rows):
    with ExitStack() as ctx:
        def sb(name, shape, dt=fp32):
            return ctx.enter_context(nc.sbuf_tensor("la_" + name, shape, dt))

        def sem(name):
            return nc.alloc_semaphore("la_" + name)

        w = sb("w", [P, C, 3 * D])
        w_o = sb("wo", [P, C, D])
        w16 = sb("w16", [P, 2, C, 3 * D], fp16)
        w_o16 = sb("wo16", [P, 2, C, D], fp16)
        causal = sb("causal", [P, P])
        diag = sb("diag", [P, C, E, HD + 1])
        keep = sb("keep", [P, TILES])
        state = sb("state", [P, C, E, 2 * HD])
        kv = sb("kv", [P, C, E, HD + 1])
        stats, mv, veps, rstd = (sb(n, [P, 2, 6]) for n in ("stats", "mv", "veps", "rstd"))
        stats2, mv2, veps2, rstd2 = (sb(n, [P, 2, 6]) for n in ("stats2", "mv2", "veps2", "rstd2"))
        xn = sb("xn", [P, 2, D])
        xT = sb("xT", [P, 2, 2, C, P], fp16)
        ex = sb("ex", [P, 2, 2 * D])
        relu = sb("relu", [P, 2, 2 * D])
        v1 = sb("v1", [P, 2, H, 2 * HD])
        qk = sb("qk", [P, 2, 2 * D])
        stack = sb("stack", [P, 2, 2, H, 4, HD], fp16)
        qS = sb("qS", [P, 2, H // 2, P], fp16)
        kS = sb("kS", [P, 2, H // 2, P], fp16)
        qT = sb("qT", [P, 2, C, P])
        sc = sb("sc", [P, 4, 4, P])
        outT = sb("outT", [P, 2, 4, P])
        den = sb("den", [P, 2, H])
        rden = sb("rden", [P, 2, H])
        o = sb("o", [P, 2, H, HD])
        oT = sb("oT", [P, 2, 2, C, P], fp16)
        x1 = sb("x1", [P, 2, D])
        xn2 = sb("xn2", [P, 2, D])
        x2T = sb("x2T", [P, 2, 2, C, P], fp16)

        (w_loaded, consts, cfill, dfill, x_first, x_loaded) = (sem(n) for n in (
            "w_loaded", "consts", "cfill", "dfill", "x_first", "x_loaded"))
        (stats_d, mv_d, veps_d, rstd_d, xn_d, xT_p, xT_d, qk_p, v_p, ex_d, relu_d, v_d, feat_d, hi_d, lo_d,
         qS_p, kS_p, qT_p, qS_d, kS_d, qT_d, sc_p, sc_d, out_p, outT_d, o2_p, den_d, rden_d, o_d,
         oT_p, oT_d, y_p, x1_d, kv_p, kvm_d, state_d, stats2_d, mv2_d, veps2_d, rstd2_d, xn2_d,
         x2T_p, x2T_d, lg_p, lg_d, x1_s, xn2_s, st_p, w_hi, w_lo, xlo_d, olo_d, x2lo_d, wo_loaded, x_next) = (sem(n) for n in (
            "stats_d", "mv_d", "veps_d", "rstd_d", "xn_d", "xT_p", "xT_d", "qk_p", "v_p", "ex_d", "relu_d",
            "v_d", "feat_d", "hi_d", "lo_d", "qS_p", "kS_p", "qT_p", "qS_d", "kS_d", "qT_d", "sc_p", "sc_d",
            "out_p", "outT_d", "o2_p", "den_d", "rden_d", "o_d", "oT_p", "oT_d", "y_p", "x1_d", "kv_p",
            "kvm_d", "state_d", "stats2_d", "mv2_d", "veps2_d", "rstd2_d", "xn2_d", "x2T_p", "x2T_d",
            "lg_p", "lg_d", "x1_s", "xn2_s", "st_p", "w_hi", "w_lo",
            "xlo_d", "olo_d", "x2lo_d", "wo_loaded",
            "x_next"))
        X, QK, V, TQ, TK, S0, S1, O = k.bank
        SC = [S0, S1]
        XCHUNK = 4

        with nc.Block() as block:
            @block.sync
            def _(sp):
                x_view = x_in.rearrange("(t p) d -> p t d", p=P)
                sp.dma_start(k.x[:, 0:1, :], x_view[:, 0:1, :]).then_inc(x_first, 16)
                for n, wx in enumerate((wq, wk, wv)):
                    sp.dma_start(w[:, :, n * D:(n + 1) * D], wx.rearrange("(c p) n -> p c n", p=P)).then_inc(w_loaded, 16)
                sp.dma_start(k.x[:, 1:XCHUNK, :], x_view[:, 1:XCHUNK, :]).then_inc(x_next, 16)
                sp.dma_start(w_o[:, :, :], wo.rearrange("(c p) n -> p c n", p=P)).then_inc(wo_loaded, 16)
                for g in range(1, TILES // XCHUNK):
                    sp.dma_start(k.x[:, g * XCHUNK:(g + 1) * XCHUNK, :],
                                 x_view[:, g * XCHUNK:(g + 1) * XCHUNK, :]).then_inc(x_loaded, 16)

                def slot(i, p):
                    t, q = i - 1, (p + 1) % 2
                    if active(t):
                        sp.wait_ge(x1_d, t + 1)
                        sp.dma_start(x_base[bass.ds(t * P, P), :], x1[:, q, :]).then_inc(x1_s, 16)
                        sp.wait_ge(xn2_d, t + 1)
                        sp.dma_start(rows[bass.ds(t * P, P), 0:D], xn2[:, q, :]).then_inc(xn2_s, 16)
                pipeline(sp, slot, 1, 5, 29, 32, 4, 2)
                sp.wait_ge(w_loaded, 48)
                sp.wait_ge(wo_loaded, 16)
                sp.wait_ge(x1_s, 16 * TILES)
                sp.wait_ge(xn2_s, 16 * TILES)

            @block.gpsimd
            def _(pool):
                pool.memset(causal[:, :], 1.0).then_inc(cfill, 1)
                pool.memset(diag[:, :, :, :], 1.0).then_inc(cfill, 1)
                pool.wait_ge(cfill, 2)
                pool.affine_select(out=causal[:, :], in_=causal[:, :], compare_op=ALU.is_ge, fill=0.0,
                                   base=0, pattern=[[1, P]], channel_multiplier=-1).then_inc(cfill, 1)
                halves = diag[:, 0, :, :].rearrange("p (b j) n -> p b j n", b=2)
                pool.affine_select(out=halves, in_=halves, compare_op=ALU.is_ge, fill=0.0,
                                   base=0, pattern=[[-HD, 2], [-2 * HD, 4], [0, HD + 1]],
                                   channel_multiplier=1).then_inc(cfill, 1)
                pool.wait_ge(cfill, 4)
                pool.affine_select(out=halves, in_=halves, compare_op=ALU.is_ge, fill=0.0,
                                   base=HD - 1, pattern=[[HD, 2], [2 * HD, 4], [0, HD + 1]],
                                   channel_multiplier=-1).then_inc(cfill, 1)
                pool.wait_ge(cfill, 5)
                pool.tensor_copy(diag[:, 1, :, :], diag[:, 0, :, :]).then_inc(consts, 1)

                def slot(i, p):
                    t, q = i + 3, (p + 1) % 2
                    if active(t):
                        pool.wait_ge(mv_d, t + 1)
                        pool.tensor_tensor(veps[:, q, 0:1], mv[:, q, 1:2], k.eps[:, :], ALU.add).then_inc(veps_d, 1)
                        pool.wait_ge(veps_d, t + 1)
                        pool.tensor_tensor(rstd[:, q, 0:1], veps[:, q, 0:1], k.half[:, :], ALU.pow).then_inc(rstd_d, 1)
                    t, q = i - 1, (p + 1) % 2
                    if active(t):
                        pool.wait_ge(mv2_d, t + 1)
                        pool.tensor_tensor(veps2[:, q, 0:1], mv2[:, q, 1:2], k.eps[:, :], ALU.add).then_inc(veps2_d, 1)
                        pool.wait_ge(veps2_d, t + 1)
                        pool.tensor_tensor(rstd2[:, q, 0:1], veps2[:, q, 0:1], k.half[:, :], ALU.pow).then_inc(rstd2_d, 1)
                pipeline(pool, slot, -3, 5, 29, 32, 4, 2)

            @block.vector
            def _(dve):
                dve.memset(state[:, :, :, :], 0.0).then_inc(dfill, 1)
                dve.memset(keep[:, :], 1.0).then_inc(dfill, 1)
                dve.memset(v1[:, :, :, HD:2 * HD], 1.0).then_inc(dfill, 1)
                dve.memset(stack[:, :, :, :, 3, :].rearrange("p q n h d -> p (q n) h d"), 0.0).then_inc(dfill, 1)
                dve.wait_ge(dfill, 4)
                dve.memset(keep[:, SEQ_TILES - 1:SEQ_TILES], 0.0).then_inc(consts, 1)
                dve.wait_ge(consts, 2)

                def slot(i, p):
                    t, q = i + 3, (p + 1) % 2
                    if active(t):
                        dve.wait_ge(x_first, 16)
                        if later(t, 1):
                            dve.wait_ge(x_next, 16)
                        if later(t, XCHUNK):
                            dve.wait_ge(x_loaded, 16 * (TILES // XCHUNK - 1))
                        dve.bn_stats(stats[:, q, 0:6], k.x[:, bass.ds(t, 1), :].squeeze(1)).then_inc(stats_d, 1)
                        dve.wait_ge(stats_d, t + 1)
                    t, q = i - 2, p
                    if active(t):
                        dve.wait_ge(rstd2_d, t + 1)
                        dve.wait_ge(mv2_d, t + 1)
                        if later(t, 2):
                            dve.wait_ge(x2T_p, t - 1)
                        if later(t, 1):
                            dve.wait_ge(xn2_s, t * 16)
                        dve.tensor_scalar(xn2[:, q, :], x1[:, q, :], mv2[:, q, 0:1],
                                          rstd2[:, q, 0:1], ALU.subtract, ALU.mult).then_inc(xn2_d, 1)
                    t, q = i + 3, (p + 1) % 2
                    if active(t):
                        dve.bn_aggr(mv[:, q, 0:2], stats[:, q, 0:6]).then_inc(mv_d, 1)
                    t, q = i + 1, (p + 1) % 2
                    if active(t):
                        dve.wait_ge(relu_d, t + 1)
                        if later(t, 2):
                            dve.wait_ge(kv_p, t - 1)
                            dve.wait_ge(qT_p, t - 1)
                        dve.scalar_tensor_tensor(qk[:, q, :], ex[:, q, :], 1.0, relu[:, q, :], ALU.min,
                                                 ALU.add).then_inc(feat_d, 1)
                    t, q = i, p
                    if active(t):
                        masked_scores(t, 0)
                    t, q = i, p
                    if active(t):
                        masked_scores(t, 1)
                    t, q = i - 1, (p + 1) % 2
                    if active(t):
                        o2 = TQ[:, :].rearrange("p (h c) -> p h c", h=H)
                        dve.wait_ge(o2_p, t + 1)
                        dve.tensor_scalar(den[:, q, :], o2[:, :, HD], EPS_DEN, None, ALU.add).then_inc(den_d, 1)
                        dve.wait_ge(den_d, t + 1)
                        dve.reciprocal(rden[:, q, :], den[:, q, :]).then_inc(rden_d, 1)
                        dve.wait_ge(rden_d, t + 1)
                        dve.tensor_tensor(o[:, q, :, :], o2[:, :, 0:HD],
                                          rden[:, q, :].unsqueeze(2).broadcast_to([P, H, HD]), ALU.mult).then_inc(o_d, 1)
                    t, q = i + 2, p
                    if active(t):
                        dve.wait_ge(xT_d, t + 1)
                        dve.tensor_tensor(xT[:, q, 1, :, :], X[:, 0:D].rearrange("p (c t) -> p c t", c=C),
                                          xT[:, q, 0, :, :], ALU.subtract).then_inc(xlo_d, 1)
                    t, q = i, p
                    if active(t):
                        masked_scores(t, 2)
                    t, q = i - 1, (p + 1) % 2
                    if active(t):
                        dve.wait_ge(oT_d, t + 1)
                        dve.tensor_tensor(oT[:, q, 1, :, :], TQ[:, 0:D].rearrange("p (c t) -> p c t", c=C),
                                          oT[:, q, 0, :, :], ALU.subtract).then_inc(olo_d, 1)
                    t, q = i + 1, (p + 1) % 2
                    if active(t):
                        dve.wait_ge(feat_d, t + 1)
                        if later(t, 2):
                            dve.wait_ge(qS_p, t - 1)
                            dve.wait_ge(kS_p, t - 1)
                        qv = qk[:, q, :].rearrange("p (n h d) -> p n h d", n=2, h=H)
                        dve.tensor_copy(stack[:, q, 0, :, 0:2, :],
                                        qv[:, 0, :, :].unsqueeze(2).broadcast_to([P, H, 2, HD])).then_inc(hi_d, 1)
                    t, q = i, p
                    if active(t):
                        dve.wait_ge(kv_p, t + 1)
                        kvp = V[:, 0:C * E * (HD + 1)].rearrange("p (c h n) -> p (c h) n", c=C, h=E)
                        dve.scalar_tensor_tensor(kv[:, :, :, :].rearrange("p c h n -> p (c h) n"), kvp,
                                                 keep[:, bass.ds(t, 1)],
                                                 diag[:, :, :, :].rearrange("p c h n -> p (c h) n"),
                                                 ALU.mult, ALU.mult).then_inc(kvm_d, 1)
                    t, q = i, p
                    if active(t):
                        masked_scores(t, 3)
                    t, q = i + 1, (p + 1) % 2
                    if active(t):
                        qv = qk[:, q, :].rearrange("p (n h d) -> p n h d", n=2, h=H)
                        dve.wait_ge(hi_d, (t + 1) * 2)
                        dve.tensor_tensor(stack[:, q, 0, :, 2, :], qv[:, 0, :, :], stack[:, q, 0, :, 0, :],
                                          ALU.subtract).then_inc(lo_d, 1)
                        dve.tensor_tensor(stack[:, q, 1, :, 1, :], qv[:, 1, :, :], stack[:, q, 1, :, 0, :],
                                          ALU.subtract).then_inc(lo_d, 1)
                    t, q = i - 2, p
                    if active(t):
                        dve.wait_ge(x2T_d, t + 1)
                        dve.tensor_tensor(x2T[:, q, 1, :, :], X[:, 0:D].rearrange("p (c t) -> p c t", c=C),
                                          x2T[:, q, 0, :, :], ALU.subtract).then_inc(x2lo_d, 1)
                    t, q = i - 1, (p + 1) % 2
                    if active(t):
                        if later(t, 1):
                            dve.wait_ge(x1_s, t * 16)
                        dve.wait_ge(y_p, t + 1)
                        dve.scalar_tensor_tensor(x1[:, q, :], TQ[:, 0:D], 1 / WS,
                                                 k.x[:, bass.ds(t, 1), :].squeeze(1), ALU.mult, ALU.add).then_inc(x1_d, 1)
                    t, q = i - 1, (p + 1) % 2
                    if active(t):
                        dve.wait_ge(x1_d, t + 1)
                        dve.bn_stats(stats2[:, q, 0:6], x1[:, q, :]).then_inc(stats2_d, 1)
                        dve.wait_ge(stats2_d, t + 1)
                    t, q = i, p
                    if active(t):
                        dve.wait_ge(kvm_d, t + 1)
                        dve.wait_ge(st_p, t + 1)
                        sv = state[:, :, :, 0:HD + 1].rearrange("p c h n -> p (c h) n")
                        dve.scalar_tensor_tensor(sv, sv, keep[:, bass.ds(t, 1)],
                                                 kv[:, :, :, :].rearrange("p c h n -> p (c h) n"),
                                                 ALU.mult, ALU.add).then_inc(state_d, 1)
                    t, q = i - 1, (p + 1) % 2
                    if active(t):
                        dve.bn_aggr(mv2[:, q, 0:2], stats2[:, q, 0:6]).then_inc(mv2_d, 1)
                    t, q = i + 3, (p + 1) % 2
                    if active(t):
                        dve.wait_ge(rstd_d, t + 1)
                        dve.wait_ge(mv_d, t + 1)
                        if later(t, 2):
                            dve.wait_ge(xT_p, t - 1)
                        dve.tensor_scalar(xn[:, q, :], k.x[:, bass.ds(t, 1), :].squeeze(1), mv[:, q, 0:1],
                                          rstd[:, q, 0:1], ALU.subtract, ALU.mult).then_inc(xn_d, 1)

                def masked_scores(t, g):
                    dve.wait_ge(sc_p, t * 4 + (g + 1))
                    if later(t, 1):
                        dve.wait_ge(out_p, t)
                    dve.tensor_tensor(sc[:, g, :, :], SC[g % 2][:, :].rearrange("p (h t) -> p h t", t=P),
                                      causal[:, :].unsqueeze(1).broadcast_to([P, 4, P]), ALU.mult).then_inc(sc_d, 1)

                slot(-3, 1)
                dve.wait_ge(w_hi, 2)
                dve.scalar_tensor_tensor(w16[:, 1, :, :], w[:, :, :], WS, w16[:, 0, :, :], ALU.mult,
                                         ALU.subtract).then_inc(w_lo, 1)
                dve.scalar_tensor_tensor(w_o16[:, 1, :, :], w_o[:, :, :], WS, w_o16[:, 0, :, :], ALU.mult,
                                         ALU.subtract).then_inc(w_lo, 1)
                pipeline(dve, slot, -2, 5, 29, 33, 4, 2)

            @block.scalar
            def _(act):
                act.wait_ge(w_loaded, 48)
                act.activation(w16[:, 0, :, :], w[:, :, :], ACT.Copy, scale=WS).then_inc(w_hi, 1)
                act.wait_ge(wo_loaded, 16)
                act.activation(w_o16[:, 0, :, :], w_o[:, :, :], ACT.Copy, scale=WS).then_inc(w_hi, 1)
                act.wait_ge(consts, 2)

                def slot(i, p):
                    t, q = i + 1, (p + 1) % 2
                    if active(t):
                        act.wait_ge(qk_p, t + 1)
                        if later(t, 2):
                            act.wait_ge(feat_d, t - 1)
                        act.activation(ex[:, q, :], QK[:, :], ACT.Exp, scale=1 / WS).then_inc(ex_d, 1)
                        act.activation(relu[:, q, :], QK[:, :], ACT.Relu, scale=1 / WS).then_inc(relu_d, 1)
                        act.wait_ge(v_p, t + 1)
                        if later(t, 2):
                            act.wait_ge(kv_p, t - 1)
                            act.wait_ge(out_p, t - 1)
                        act.activation(v1[:, q, :, 0:HD], V[:, 0:D].rearrange("p (h d) -> p h d", h=H), ACT.Copy, scale=1 / WS).then_inc(v_d, 1)
                    t, q = i + 2, p
                    if active(t):
                        act.wait_ge(xT_p, t + 1)
                        if later(t, 2):
                            act.wait_ge(v_p, t - 1)
                        act.activation(xT[:, q, 0, :, :], X[:, 0:D].rearrange("p (c t) -> p c t", c=C), ACT.Copy).then_inc(xT_d, 1)
                    t, q = i + 1, (p + 1) % 2
                    if active(t):
                        act.wait_ge(feat_d, t + 1)
                        if later(t, 2):
                            act.wait_ge(kS_p, t - 1)
                        act.activation(stack[:, q, 1, :, 0:3:2, :],
                                       qk[:, q, D:2 * D].rearrange("p (h d) -> p h d", h=H).unsqueeze(2).broadcast_to([P, H, 2, HD]),
                                       ACT.Copy).then_inc(hi_d, 1)
                    t, q = i - 1, (p + 1) % 2
                    if active(t):
                        act.wait_ge(oT_p, t + 1)
                        if later(t, 2):
                            act.wait_ge(y_p, t - 1)
                        act.activation(oT[:, q, 0, :, :], TQ[:, 0:D].rearrange("p (c t) -> p c t", c=C), ACT.Copy).then_inc(oT_d, 1)
                    t, q = i - 2, p
                    if active(t):
                        act.wait_ge(x2T_p, t + 1)
                        if later(t, 2):
                            act.wait_ge(lg_p, t - 1)
                        act.activation(x2T[:, q, 0, :, :], X[:, 0:D].rearrange("p (c t) -> p c t", c=C), ACT.Copy).then_inc(x2T_d, 1)
                    t, q = i, p
                    if active(t):
                        act.wait_ge(out_p, t + 1)
                        if later(t, 2):
                            act.wait_ge(o2_p, t - 1)
                        act.activation(outT[:, q, :, :], O[:, :].rearrange("p (g t) -> p g t", g=4), ACT.Copy).then_inc(outT_d, 1)
                    t, q = i + 1, (p + 1) % 2
                    if active(t):
                        act.wait_ge(qT_p, t + 1)
                        act.activation(qT[:, q, :, :], V[:, 0:D].rearrange("p (c t) -> p c t", c=C), ACT.Copy).then_inc(qT_d, 1)
                        act.wait_ge(kS_p, t + 1)
                        if later(t, 2):
                            act.wait_ge(out_p, t - 1)
                        act.activation(kS[:, q, :, :], TK[:, :].bitcast(fp16).rearrange("p (h t) -> p h t", t=P), ACT.Copy).then_inc(kS_d, 1)
                    t, q = i - 2, p
                    if active(t):
                        act.wait_ge(lg_p, t + 1)
                        act.activation(k.logits[:, bass.ds(t, 1), :].squeeze(1), X[:, 0:E], ACT.Copy, scale=1 / WS).then_inc(lg_d, 1)
                    t, q = i + 1, (p + 1) % 2
                    if active(t):
                        act.wait_ge(qS_p, t + 1)
                        if later(t, 2):
                            act.wait_ge(out_p, t - 1)
                        act.activation(qS[:, q, :, :], TQ[:, :].bitcast(fp16).rearrange("p (h t) -> p h t", t=P), ACT.Copy).then_inc(qS_d, 1)
                pipeline(act, slot, -2, 5, 29, 33, 4, 2)

            @block.tensor
            def _(pe):
                pe.wait_ge(consts, 2)

                def transpose2(bank, src, done):
                    for c in range(C):
                        last = pe.transpose(bank[:, c * P:(c + 1) * P], src[:, c * P:(c + 1) * P], k.ident[:, :])
                    last.then_inc(done, 1)

                def scores(t, q, g):
                    if g < 2:
                        if later(t, 1):
                            pe.wait_ge(sc_d, t * 4 + (g - 1))
                    else:
                        pe.wait_ge(sc_d, t * 4 + (g - 1))
                    r = 64 * (g % 2)
                    for j in range(4):
                        h = head(g, j)
                        last = pe.matmul(SC[g % 2][:, j * P:(j + 1) * P], kS[r:r + 64, q, h // 2, :],
                                         qS[r:r + 64, q, h // 2, :], start=True, stop=True)
                    last.then_inc(sc_p, 1)

                def attend(t, q, g):
                    pe.wait_ge(sc_d, t * 4 + (g + 1))
                    for j in range(4):
                        last = pe.matmul(O[32 * j:32 * j + 32, g * P:(g + 1) * P], v1[:, q, 4 * g + j, :],
                                         sc[:, g, j, :], start=False, stop=True, skip_group_check=True)
                    return last

                def slot(i, p):
                    t, q = i + 1, (p + 1) % 2
                    if active(t):
                        pe.wait_ge(xlo_d, t + 1)
                        if later(t, 1):
                            pe.wait_ge(relu_d, t)
                            pe.wait_ge(qT_d, t)
                        split_product(pe, QK[:, :], xT[:, q, :, :, :], w16[:, :, :, 0:2 * D]).then_inc(qk_p, 1)
                        split_product(pe, V[:, 0:D], xT[:, q, :, :, :], w16[:, :, :, 2 * D:3 * D]).then_inc(v_p, 1)
                    t, q = i, p
                    if active(t):
                        pe.wait_ge(qT_d, t + 1)
                        if later(t, 1):
                            pe.wait_ge(state_d, t)
                            pe.wait_ge(outT_d, t)
                        for g in range(4):
                            last = pe.matmul(O[:, g * P:(g + 1) * P], state[:, g // 2, 4 * (g % 2):4 * (g % 2) + 4, :].rearrange("p h n -> p (h n)"),
                                             qT[:, q, g // 2, :], start=(g == 0), stop=True, skip_group_check=True)
                        last.then_inc(st_p, 1)
                    t, q = i + 2, p
                    if active(t):
                        pe.wait_ge(xn_d, t + 1)
                        if later(t, 5):
                            pe.wait_ge(lg_d, t - 4)
                        elif t > 0:
                            pe.wait_ge(xlo_d, t)
                        transpose2(X, xn[:, q, :], xT_p)
                    t, q = i, p
                    if active(t):
                        pe.wait_ge(qS_d, t + 1)
                        pe.wait_ge(kS_d, t + 1)
                        scores(t, q, 0)
                        scores(t, q, 1)
                    t, q = i - 1, (p + 1) % 2
                    if active(t):
                        pe.wait_ge(outT_d, t + 1)
                        if active(i):
                            pe.wait_ge(qS_d, t + 2)
                        else:
                            pe.wait_ge(x1_d, t)
                        for g in range(4):
                            last = pe.transpose(TQ[:, g * P:(g + 1) * P], outT[:, q, g, :], k.ident[:, :])
                        last.then_inc(o2_p, 1)
                    t, q = i, p
                    if active(t):
                        pe.wait_ge(v_d, t + 1)
                        attend(t, q, 0)
                        scores(t, q, 2)
                    t, q = i, p
                    if active(t):
                        if active(i + 1):
                            pe.wait_ge(v_d, t + 2)
                        for c in range(C):
                            last = pe.matmul(V[:, c * E * (HD + 1):(c + 1) * E * (HD + 1)].rearrange("p (h n) -> p h n", h=E),
                                             qk[:, q, D + c * P:D + (c + 1) * P],
                                             v1[:, q, c * E:(c + 1) * E, 0:HD + 1], start=True, stop=True)
                        last.then_inc(kv_p, 1)
                    t, q = i, p
                    if active(t):
                        attend(t, q, 1)
                        scores(t, q, 3)
                    t, q = i - 1, (p + 1) % 2
                    if active(t):
                        pe.wait_ge(o_d, t + 1)
                        transpose2(TQ, o[:, q, :, :].rearrange("p h d -> p (h d)"), oT_p)
                    t, q = i - 2, p
                    if active(t):
                        pe.wait_ge(xn2_d, t + 1)
                        if active(i + 2):
                            pe.wait_ge(xlo_d, t + 5)
                        else:
                            pe.wait_ge(lg_d, t)
                        transpose2(X, xn2[:, q, :], x2T_p)
                    t, q = i, p
                    if active(t):
                        attend(t, q, 2)
                    t, q = i - 1, (p + 1) % 2
                    if active(t):
                        pe.wait_ge(olo_d, t + 1)
                        split_product(pe, TQ[:, 0:D], oT[:, q, :, :, :], w_o16[:, :, :, :]).then_inc(y_p, 1)
                    t, q = i + 1, (p + 1) % 2
                    if active(t):
                        pe.wait_ge(feat_d, t + 1)
                        if later(t, 1):
                            pe.wait_ge(kvm_d, t)
                        else:
                            pe.wait_ge(v_d, 1)
                        transpose2(V, qk[:, q, 0:D], qT_p)
                    t, q = i, p
                    if active(t):
                        attend(t, q, 3).then_inc(out_p, 1)
                    t, q = i + 1, (p + 1) % 2
                    if active(t):
                        pe.wait_ge(lo_d, (t + 1) * 2)
                        if later(t, 1):
                            pe.wait_ge(kS_d, t)
                        for h in range(H // 2):
                            last = pe.transpose(TK[:, :].bitcast(fp16)[:, h * P:(h + 1) * P],
                                                stack[:, q, 1, 2 * h:2 * h + 2, :, :].rearrange("p h n d -> p (h n d)"), k.ident16[:, :])
                        last.then_inc(kS_p, 1)
                        if later(t, 2):
                            pe.wait_ge(x1_d, t - 1)
                        elif t == 1:
                            pe.wait_ge(qS_d, 1)
                        for h in range(H // 2):
                            last = pe.transpose(TQ[:, :].bitcast(fp16)[:, h * P:(h + 1) * P],
                                                stack[:, q, 0, 2 * h:2 * h + 2, :, :].rearrange("p h n d -> p (h n d)"), k.ident16[:, :])
                        last.then_inc(qS_p, 1)
                    t, q = i - 2, p
                    if active(t):
                        pe.wait_ge(x2lo_d, t + 1)
                        split_product(pe, X[:, 0:E], x2T[:, q, :, :, :], k.wg16[:, :, :, :], all_terms=True).then_inc(lg_p, 1)
                slot(-2, 0)
                pe.wait_ge(w_lo, 2)
                pipeline(pe, slot, -1, 5, 29, 33, 4, 2)



def router(nc, k, name, rows, window=None):
    THRESHOLD = 0.9
    OUTSIDE = -16.0
    FAR = float(N)
    with ExitStack() as ctx:
        def sb(n, shape, dt=fp32):
            return ctx.enter_context(nc.sbuf_tensor(f"{name}_{n}", shape, dt))

        def sem(n):
            return nc.alloc_semaphore(f"{name}_{n}")

        block16 = sb("block16", [P, P], bf16)
        before16 = sb("before16", [P, P], bf16)
        token = sb("token", [P, 2, E, GROUPS], fp16)
        token_i = sb("token_i", [P, 2, E, GROUPS], i32)
        mx = sb("mx", [P, TILES])
        shifted = sb("shifted", [P, TILES, E])
        exps = sb("exps", [P, TILES, E])
        total = sb("total", [P, TILES])
        inv = sb("inv", [P, TILES])
        prob = sb("prob", [P, TILES, E])
        ahead = sb("ahead", [P, TILES, E, E])
        mass = sb("mass", [P, TILES, E, E])
        rank = sb("rank", [P, TILES, E])
        four = sb("four", [P, TILES, E, E // 2])
        two = sb("two", [P, TILES, E, E // 4])
        ahead_sum = sb("ahead_sum", [P, TILES, E])
        chosen = sb("chosen", [P, TILES, E])
        gap = sb("gap", [P, TILES, E])
        outside = sb("outside", [P, TILES, E])
        score = sb("score", [P, TILES, E])
        key_t = sb("key_t", [P, 2, E, GROUPS])
        key = sb("key", [P, GT])
        hits = sb("hits", [P, 3, GT], bf16)
        count = sb("count", [P, 3], bf16)
        floor, passed = (sb(n, [P, 1]) for n in ("floor", "passed"))
        cand, passes = (sb(n, [P, 3]) for n in ("cand", "passes"))
        units = sb("units", [P, ROUNDS + 1, 3])
        above = sb("above", [P, GT])
        equal = sb("equal", [P, GT])
        zeros = sb("zeros", [P, GT])
        scan = sb("scan", [P, GT])
        need = sb("need", [P, 1])
        offset = sb("offset", [P, 2])
        ties = sb("ties", [P, GT])
        kept = sb("kept", [P, GT])
        place = sb("place", [P, GT])
        place_t = sb("place_t", [P, GT], i32)
        parts = sb("parts", [P, 2, GT], i32)
        hi = sb("hi", [P, GT], fp16)
        lo = sb("lo", [P, GT], fp16)
        is_hi = sb("is_hi", [P, SLOT_HI, GT], fp16)
        lo_token = sb("lo_token", [P, SLOT_LO, GT], fp16)

        v, fill, consts, exps_d, key_p, count_d, sum_p, place_p, onehot_d, list_p, score_s, keyt_d, placed = (
            sem(n) for n in ("v", "fill", "consts", "exps_d", "key_p", "count_d", "sum_p", "place_p", "onehot_d",
                             "list_p", "score_s", "keyt_d", "placed"))
        shift_d, score_d, masks_d, units_d, ahead_d, rank_d = (sem(n) for n in (
            "shift_d", "score_d", "masks_d", "units_d", "ahead_d", "rank_d"))
        w_loaded, w_hi, w_lo = sem("w_loaded"), sem("w_hi"), sem("w_lo")
        KEY, SUM, PLACE, LIST = k.bank[0:4]
        by_tile = "p j e t -> p t j e"

        with nc.Block() as block:
            @block.gpsimd
            def _(pool):
                pool.memset(ahead[:, :, :, :], 0.0).then_inc(ahead_d, 1)
                for n in range(ROUNDS + 1):
                    for m in range(3):
                        pool.memset(units[:, n, m:m + 1], (m + 1) * 4.0 ** (1 - n)).then_inc(units_d, 1)
                pool.memset(block16[:, :], 1.0).then_inc(fill, 1)
                pool.memset(before16[:, :], 1.0).then_inc(fill, 1)
                pool.iota(token_i[:, :, :, :], pattern=[[P, 2], [0, E], [2 * P, GROUPS]], base=-(N // 2),
                          channel_multiplier=1).then_inc(fill, 1)
                pool.wait_ge(fill, 3)
                for n, m in enumerate((block16, before16)):
                    mv = m[:, :].rearrange("p (e g) -> p e g", e=E)
                    pool.affine_select(out=mv, in_=mv, compare_op=ALU.is_ge, fill=0.0, base=0,
                                       pattern=[[-GROUPS, E], [0, GROUPS]], channel_multiplier=1).then_inc(fill, 1)
                    pool.wait_ge(fill, 4 + 2 * n)
                    if n == 0:
                        pool.affine_select(out=mv, in_=mv, compare_op=ALU.is_ge, fill=0.0, base=GROUPS - 1,
                                           pattern=[[GROUPS, E], [0, GROUPS]], channel_multiplier=-1).then_inc(fill, 1)
                    else:
                        pool.affine_select(out=mv, in_=mv, compare_op=ALU.is_gt, fill=0.0, base=0,
                                           pattern=[[GROUPS, E], [1, GROUPS]], channel_multiplier=-1).then_inc(fill, 1)
                    pool.wait_ge(fill, 5 + 2 * n)
                pool.tensor_copy(token[:, :, :, :], token_i[:, :, :, :]).then_inc(consts, 1)
                pool.wait_ge(v, AHEAD)
                pool.tensor_tensor(four[:, :, :, :], ahead[:, :, :, 0:E // 2], ahead[:, :, :, E // 2:E], ALU.add).then_inc(rank_d, 1)
                pool.wait_ge(rank_d, 1)
                pool.tensor_tensor(two[:, :, :, :], four[:, :, :, 0:E // 4], four[:, :, :, E // 4:E // 2], ALU.add).then_inc(rank_d, 1)
                pool.wait_ge(rank_d, 2)
                pool.tensor_tensor(rank[:, :, :], two[:, :, :, 0], two[:, :, :, 1], ALU.add).then_inc(rank_d, 1)
                if window:
                    window_masks(k, pool, masks_d)
                    pool.wait_ge(w_hi, 3)
                    for split, whole in ((k.w16, k.w), (k.w_g16, k.w_g), (k.w_p16, k.w_p)):
                        for c in range(C):
                            pool.tensor_scalar(whole[:, c, :], whole[:, c, :], WS, None, ALU.mult).then_inc(w_lo, 1)
                    pool.wait_ge(w_lo, 3 * C)
                    for split, whole in ((k.w16, k.w), (k.w_g16, k.w_g), (k.w_p16, k.w_p)):
                        pool.tensor_tensor(split[:, 1, :, :], whole[:, :, :], split[:, 0, :, :], ALU.subtract).then_inc(w_lo, 1)
                    pool.wait_ge(w_lo, 3 * C + 3)

            @block.sync
            def _(sp):
                if window:
                    wqk, bqk, w_gate, b_gate, w_proj, b_proj = window
                    for dst, src in ((k.w, wqk), (k.w_g, w_gate), (k.w_p, w_proj)):
                        sp.dma_start(dst[:, :, :], src.rearrange("(c p) n -> p c n", p=P)).then_inc(w_loaded, 16)
                    for dst, src in ((k.b_qk, bqk), (k.b_g, b_gate), (k.b_p, b_proj)):
                        sp.dma_start(dst[:, :], src.partition_broadcast(P)).then_inc(w_loaded, 16)
                    sp.wait_ge(w_loaded, 6 * 16)
                sp.wait_ge(score_d, 1)
                sp.dma_start(rows[:, D:ROW].rearrange("(t p) e -> p t e", p=P), score[:, :, :]).then_inc(score_s, 16)
                sp.wait_ge(score_s, 16)

            @block.scalar
            def _(act):
                act.wait_ge(shift_d, 1)
                act.activation(exps[:, :, :], shifted[:, :, :], ACT.Exp).then_inc(exps_d, 1)
                if window:
                    act.wait_ge(w_loaded, 6 * 16)
                    for split, whole in ((k.w16, k.w), (k.w_g16, k.w_g), (k.w_p16, k.w_p)):
                        act.activation(split[:, 0, :, :], whole[:, :, :], ACT.Copy, scale=WS).then_inc(w_hi, 1)

            @block.tensor
            def _(pe):
                pe.wait_ge(keyt_d, 1)
                for j in range(2):
                    last = pe.transpose(KEY[:, j * P:(j + 1) * P], key_t[:, j, :, :].rearrange("p e t -> p (e t)"), k.ident[:, :])
                last.then_inc(key_p, 1)
                pe.wait_ge(consts, 1)
                with pe.Fori(0, ROUNDS // ROUNDS_UNROLLED) as n:
                    for u in range(ROUNDS_UNROLLED):
                        pe.wait_ge(count_d, n * ROUNDS_UNROLLED + (u + 1))
                        pe.matmul(SUM[:, 0:3], block16[:, :], count[:, :], start=True, stop=True).then_inc(sum_p, 1)
                pe.wait_ge(count_d, ROUNDS + 1)
                pe.matmul(SUM[:, 0:1], block16[:, :], count[:, 0:1], start=True, stop=True).then_inc(sum_p, 1)
                for n in (2, 3):
                    pe.wait_ge(count_d, ROUNDS + n)
                    pe.matmul(SUM[:, 0:1], before16[:, :], count[:, 0:1], start=True, stop=True).then_inc(sum_p, 1)
                pe.wait_ge(v, PLACED)
                for j in range(2):
                    last = pe.transpose(PLACE[:, j * P:(j + 1) * P], place[:, j * P:(j + 1) * P], k.ident[:, :])
                last.then_inc(place_p, 1)
                pe.wait_ge(onehot_d, 1)
                for e in range(E):
                    for n in range(TILES):
                        c = (n // GROUPS) * P + e * GROUPS + n % GROUPS
                        last = pe.matmul(LIST[0:SLOT_HI, e * SLOT_LO:(e + 1) * SLOT_LO], is_hi[:, :, c], lo_token[:, :, c],
                                         start=(n == 0), stop=(n == TILES - 1))
                last.then_inc(list_p, 1)

            @block.vector
            def _(dve):
                done = [0]

                def link(ins):
                    done[0] += 1
                    ins.then_inc(v, 1)
                    dve.wait_ge(v, done[0])

                wide = [P, TILES, E]
                dve.memset(zeros[:, :], 0.0)
                link(dve.memset(floor[:, :], OUTSIDE))
                link(dve.reduce_max(mx[:, :], k.logits[:, :, :], AX.X))
                dve.tensor_tensor(shifted[:, :, :], k.logits[:, :, :], mx[:, :].unsqueeze(2).broadcast_to(wide),
                                  ALU.subtract).then_inc(shift_d, 1)
                dve.wait_ge(exps_d, 1)
                link(dve.reduce_sum(total[:, :], exps[:, :, :], AX.X))
                link(dve.reciprocal(inv[:, :], total[:, :]))
                link(dve.tensor_tensor(prob[:, :, :], exps[:, :, :], inv[:, :].unsqueeze(2).broadcast_to(wide), ALU.mult))
                dve.wait_ge(ahead_d, 1)
                for e in range(E):
                    if e:
                        last = dve.tensor_tensor(ahead[:, :, e, 0:e], prob[:, :, 0:e],
                                                 prob[:, :, e:e + 1].broadcast_to([P, TILES, e]), ALU.is_ge)
                    if e < E - 1:
                        last = dve.tensor_tensor(ahead[:, :, e, e + 1:E], prob[:, :, e + 1:E],
                                                 prob[:, :, e:e + 1].broadcast_to([P, TILES, E - 1 - e]), ALU.is_gt)
                link(last)
                assert done[0] == AHEAD, done[0]
                link(dve.tensor_tensor(mass[:, :, :, :], ahead[:, :, :, :],
                                       prob[:, :, :].unsqueeze(2).broadcast_to([P, TILES, E, E]), ALU.mult))
                link(dve.reduce_sum(ahead_sum[:, :, :], mass[:, :, :, :], AX.X))
                link(dve.tensor_scalar(chosen[:, :, :], ahead_sum[:, :, :], THRESHOLD, None, ALU.is_lt))
                dve.tensor_scalar(outside[:, :, :], chosen[:, :, :], -1.0, -OUTSIDE, ALU.add, ALU.mult)
                dve.wait_ge(rank_d, 3)
                link(dve.scalar_tensor_tensor(gap[:, :, :], rank[:, :, :], 1.0, prob[:, :, :], ALU.add, ALU.subtract))
                link(dve.tensor_tensor(gap[:, :, :], gap[:, :, :], chosen[:, :, :], ALU.mult))
                split = "p (t j) e -> p t j e"
                dve.tensor_tensor(key_t[:, :, :, :].rearrange(by_tile), outside[:, :, :].rearrange(split, j=2),
                                  gap[:, :, :].rearrange(split, j=2), ALU.subtract).then_inc(keyt_d, 1)
                dve.tensor_tensor(score[:, :, :], prob[:, :, :], chosen[:, :, :], ALU.mult).then_inc(score_d, 1)
                dve.wait_ge(key_p, 1)
                link(dve.tensor_copy(key[:, :], KEY[:, 0:GT]))
                dve.wait_ge(units_d, 3 * (ROUNDS + 1))
                link(dve.tensor_scalar(cand[:, :], units[:, 0, :], floor[:, :], None, ALU.add))
                with dve.Fori(0, ROUNDS // ROUNDS_UNROLLED) as n:
                    for u in range(ROUNDS_UNROLLED):
                        at = n * (3 * ROUNDS_UNROLLED) + (done[0] + 3 * u)
                        rnd = n * ROUNDS_UNROLLED + u
                        dve.wait_ge(v, at)
                        for m in range(3):
                            last = dve.tensor_scalar(hits[:, m, :], key[:, :], cand[:, m:m + 1], None, ALU.is_ge, ALU.add,
                                                     accum_out=count[:, m:m + 1])
                        last.then_inc(count_d, 1)
                        dve.wait_ge(sum_p, rnd + 1)
                        dve.tensor_scalar(passes[:, :], SUM[:, 0:3], CAP - 0.5, None, ALU.is_ge, ALU.add,
                                          accum_out=passed[:, :]).then_inc(v, 1)
                        dve.wait_ge(v, at + 1)
                        dve.scalar_tensor_tensor(floor[:, :], units[:, bass.ds(rnd, 1), 0:1].squeeze(1), passed[:, :],
                                                 floor[:, :], ALU.mult, ALU.add).then_inc(v, 1)
                        dve.wait_ge(v, at + 2)
                        dve.tensor_scalar(cand[:, :], units[:, bass.ds(rnd + 1, 1), :].squeeze(1), floor[:, :], None,
                                          ALU.add).then_inc(v, 1)
                done[0] += 3 * ROUNDS
                dve.wait_ge(v, done[0])
                dve.tensor_scalar(above[:, :], key[:, :], floor[:, :], None, ALU.is_gt, ALU.add,
                                  accum_out=count[:, 0:1]).then_inc(count_d, 1)
                link(dve.tensor_scalar(equal[:, :], key[:, :], floor[:, :], None, ALU.is_equal))
                link(dve.tensor_tensor_scan(scan[:, :], equal[:, :], zeros[:, :], 0.0, ALU.add, ALU.add))
                dve.wait_ge(sum_p, ROUNDS + 1)
                dve.tensor_scalar(need[:, :], SUM[:, 0:1], -1.0, float(CAP), ALU.mult, ALU.add)
                dve.tensor_copy(count[:, 0:1], scan[:, GT - 1:GT]).then_inc(count_d, 1)
                dve.wait_ge(sum_p, ROUNDS + 2)
                link(dve.tensor_copy(offset[:, 0:1], SUM[:, 0:1]))
                link(dve.tensor_scalar(ties[:, :], scan[:, :], offset[:, 0:1], need[:, :], ALU.add, ALU.is_le))
                link(dve.tensor_tensor(ties[:, :], ties[:, :], equal[:, :], ALU.mult))
                link(dve.tensor_tensor(kept[:, :], ties[:, :], above[:, :], ALU.add))
                link(dve.tensor_tensor_scan(scan[:, :], kept[:, :], zeros[:, :], 0.0, ALU.add, ALU.add))
                dve.tensor_copy(count[:, 0:1], scan[:, GT - 1:GT]).then_inc(count_d, 1)
                dve.wait_ge(sum_p, ROUNDS + 3)
                link(dve.tensor_copy(offset[:, 1:2], SUM[:, 0:1]))
                link(dve.tensor_scalar(scan[:, :], scan[:, :], offset[:, 1:2], FAR - 1, ALU.add, ALU.add))
                link(dve.scalar_tensor_tensor(place[:, :], kept[:, :], -FAR, scan[:, :], ALU.mult, ALU.add))
                assert done[0] == PLACED, done[0]
                dve.wait_ge(place_p, 1)
                link(dve.tensor_copy(place_t[:, :], PLACE[:, 0:GT]))
                dve.tensor_scalar(parts[:, 0, :], place_t[:, :], SLOT_LO.bit_length() - 1, None, ALU.logical_shift_right)
                link(dve.tensor_scalar(parts[:, 1, :], place_t[:, :], SLOT_LO - 1, None, ALU.bitwise_and))
                dve.tensor_copy(hi[:, :], parts[:, 0, :])
                link(dve.tensor_copy(lo[:, :], parts[:, 1, :]))
                dve.wait_ge(consts, 1)
                for c in range(SLOT_HI):
                    dve.tensor_scalar(is_hi[:, c, :], hi[:, :], float(c), None, ALU.is_equal)
                tokens = token[:, :, :, :].rearrange("p j e t -> p (j e t)")
                for c in range(SLOT_LO):
                    last = dve.scalar_tensor_tensor(lo_token[:, c, :], lo[:, :], float(c), tokens, ALU.is_equal, ALU.mult)
                last.then_inc(onehot_d, 1)
                dve.wait_ge(list_p, 1)
                by_slot = LIST[0:SLOT_HI, 0:E * SLOT_LO].rearrange("h (e l) -> h e l", e=E)
                SUB = CAP // P
                for q in range(P // SLOT_HI):
                    dve.tensor_scalar(k.index[q * SLOT_HI:(q + 1) * SLOT_HI, :, :], by_slot[:, :, q * SUB:(q + 1) * SUB],
                                      float(N // 2), None, ALU.add).then_inc(placed, 1)
                dve.wait_ge(placed, P // SLOT_HI)



def experts(nc, k, name, rows, w1t, w2t, total):
    SUB = CAP // P
    with ExitStack() as ctx:
        def sb(n, shape, dt=fp32):
            return ctx.enter_context(nc.sbuf_tensor(f"{name}_{n}", shape, dt))

        def sem(n):
            return nc.alloc_semaphore(f"{name}_{n}")

        RING = 3
        assert (E - 2) % RING == 0
        index = k.index[:, :, :].bitcast(u32)
        rowsb = sb("rows", [P, RING, SUB, ROW])
        w1 = sb("w1", [P, RING, C, F])
        w2 = sb("w2", [P, RING, FC, D])
        xT = sb("xT", [P, RING, C, CAP])
        hid = sb("hid", [P, RING, FC, CAP])
        y = sb("y", [P, RING, SUB, D])
        scatter_s, xT_p, xT_d, up_p, hid_d, down_p, y_d = (sem(n) for n in (
            "scatter_s", "xT_p", "xT_d", "up_p", "hid_d", "down_p", "y_d"))
        gather_l = [sem(f"gather_l{q}") for q in range(RING)]
        w_l = [sem(f"w_l{q}") for q in range(RING)]
        XB, UB, DB = k.bank[0:2], k.bank[2:4], k.bank[4:6]

        def over(eng, body):
            for e in range(2):
                body(e, e, 0)
            with eng.Fori(0, (E - 2) // RING) as n:
                for u in range(RING):
                    body(n * RING + (2 + u), (2 + u) % RING, n + (2 + u) // RING)

        with nc.Block() as block:
            @block.sync
            def _(sp):
                def body(e, q, turn):
                    if later(e, 2):
                        sp.wait_ge(down_p, (e - 1) * 2)
                    sp.dma_start(w1[:, q, :, :], w1t[bass.ds(e * D, D), :].rearrange("(c p) f -> p c f", p=P)).then_inc(w_l[q], 16)
                    sp.dma_start(w2[:, q, :, :], w2t[bass.ds(e * F, F), :].rearrange("(c p) d -> p c d", p=P)).then_inc(w_l[q], 16)
                over(sp, body)
                sp.wait_ge(scatter_s, E * SUB * 16)

            @block.gpsimd
            def _(pool):
                def gather(e):
                    for s in range(SUB):
                        pool.indirect_dma_start(
                            out=rowsb[:, e % RING, s, :], out_offset=None, in_=rows,
                            in_offset=bass.IndirectOffsetOnAxis(ap=index[:, e, s:s + 1], axis=0),
                            compute_op=ALU.bypass).then_inc(gather_l[e % RING], 16)

                def scatter(e, q):
                    if later(e, 1):
                        pool.wait_ge(scatter_s, e * SUB * 16)
                    for s in range(SUB):
                        if s % 2 == 0:
                            pool.wait_ge(y_d, e * 2 + (s // 2 + 1))
                        pool.indirect_dma_start(
                            out=total, out_offset=bass.IndirectOffsetOnAxis(ap=index[:, e, s:s + 1], axis=0),
                            in_=y[:, q, s, :], in_offset=None,
                            compute_op=ALU.add).then_inc(scatter_s, 16)

                for e in range(RING):
                    gather(e)
                for e in range(E):
                    scatter(e, e % RING)
                    if e + RING < E:
                        gather(e + RING)

            @block.scalar
            def _(act):
                def body(e, q, turn):
                    for c in range(C):
                        act.wait_ge(xT_p, e * C + (c + 1))
                        if later(e, 2):
                            act.wait_ge(up_p, (e - 1) * FC)
                        act.activation(xT[:, q, c, :], XB[c][:, :], ACT.Copy).then_inc(xT_d, 1)
                    for f in range(FC):
                        act.wait_ge(up_p, e * FC + (f + 1))
                        if later(e, 2):
                            act.wait_ge(down_p, (e - 1) * 2)
                        act.activation(hid[:, q, f, :], UB[f][:, :], ACT.Gelu).then_inc(hid_d, 1)
                over(act, body)

            @block.vector
            def _(dve):
                def body(e, q, turn):
                    for half in range(2):
                        dve.wait_ge(down_p, e * 2 + (half + 1))
                        if later(e, 2):
                            dve.wait_ge(scatter_s, (e - 1) * SUB * 16)
                        for s in range(2 * half, 2 * half + 2):
                            last = dve.tensor_scalar(y[:, q, s, :], DB[half][:, (s % 2) * D:(s % 2 + 1) * D],
                                                     rowsb[:, q, s, bass.ds(D + e, 1)], None, ALU.mult)
                        last.then_inc(y_d, 1)
                over(dve, body)

            @block.tensor
            def _(pe):
                def down(e, q):
                    pe.wait_ge(hid_d, (e + 1) * FC)
                    for half in range(2):
                        if later(e, 1):
                            pe.wait_ge(y_d, (e - 1) * 2 + (half + 1))
                        for s in range(2 * half, 2 * half + 2):
                            for f in range(FC):
                                last = pe.matmul(DB[half][:, (s % 2) * D:(s % 2 + 1) * D], hid[:, q, f, s * P:(s + 1) * P],
                                                 w2[:, q, f, :], start=(f == 0), stop=(f == FC - 1))
                        last.then_inc(down_p, 1)

                def body(e, q, turn):
                    pe.wait_ge(gather_l[q], (turn + 1) * SUB * 16)
                    for c in range(C):
                        if later(e, 1):
                            pe.wait_ge(xT_d, (e - 1) * C + (c + 1))
                        for s in range(SUB):
                            last = pe.transpose(XB[c][:, s * P:(s + 1) * P], rowsb[:, q, s, c * P:(c + 1) * P], k.ident[:, :])
                        last.then_inc(xT_p, 1)
                    if later(e, 1):
                        down(e - 1, (q - 1) % RING)
                    pe.wait_ge(w_l[q], (turn + 1) * 32)
                    pe.wait_ge(xT_d, (e + 1) * C)
                    for f in range(FC):
                        if later(e, 1):
                            pe.wait_ge(hid_d, (e - 1) * FC + (f + 1))
                        for c in range(C):
                            last = pe.matmul(UB[f][:, :], w1[:, q, c, f * P:(f + 1) * P], xT[:, q, c, :],
                                             start=(c == 0), stop=(c == C - 1))
                        last.then_inc(up_p, 1)
                over(pe, body)
                down(E - 1, (E - 1) % RING)



def windowed_attention(nc, k, x_in, x_base, rows):
    SCALE = float(HD) ** -0.5
    TOP = 2.0 ** 14
    with ExitStack() as ctx:
        def sb(name, shape, dt=fp32):
            return ctx.enter_context(nc.sbuf_tensor("wa_" + name, shape, dt))

        def sem(name):
            return nc.alloc_semaphore("wa_" + name)

        w16, w_g16, w_p16, b_qk, b_g, b_p = k.w16, k.w_g16, k.w_p16, k.b_qk, k.b_g, k.b_p
        mask_q, mask_k, tied_q, tied_k = k.mask_q, k.mask_k, k.tied_q, k.tied_k
        pen = sb("pen", [P, 2, TILES])
        penalty = sb("penalty", [P, 2, 2])
        stats, mv, veps, rstd = (sb(n, [P, 2, 6]) for n in ("stats", "mv", "veps", "rstd"))
        stats2, mv2, veps2, rstd2 = (sb(n, [P, 2, 6]) for n in ("stats2", "mv2", "veps2", "rstd2"))
        xn = sb("xn", [P, 2, D])
        xT = sb("xT", [P, 2, 2, C, P], fp16)
        qk = sb("qk", [P, 2, 2 * D])
        gl, gm, gex, gsum, ginv = (sb(n, [P, 4, H]) for n in ("gl", "gm", "gex", "gsum", "ginv"))
        v1 = sb("v1", [P, 4, H, 2 * HD])
        stack = sb("stack", [P, 2, 2, H, 4, HD], fp16)
        qS = sb("qS", [P, 2, H // 2, P], fp16)
        qM = sb("qM", [P, 2, H // 2, P], fp16)
        kS = sb("kS", [P, 4, H // 2, P], fp16)
        mdiag = sb("mdiag", [P, H])
        mtied = sb("mtied", [P, H])
        mfar = sb("mfar", [P, 2])
        mall = sb("mall", [P, 2, H])
        pd = sb("pd", [P, 4, 4, P])
        pt = sb("pt", [P, TIED_ALL])
        outT = sb("outT", [P, 2, 4, P])
        rden = sb("rden", [P, 2, H])
        gate = sb("gate", [P, 2, H])
        o = sb("o", [P, 2, H, HD])
        oT = sb("oT", [P, 2, 2, C, P], fp16)
        xb = sb("xb", [P, 2, D])
        x1 = sb("x1", [P, 2, D])
        xn2 = sb("xn2", [P, 2, D])
        x2T = sb("x2T", [P, 2, 2, C, P], fp16)

        NAMES = ("x_first", "x_loaded", "fill", "dfill", "consts", "stats_d", "mv_d", "veps_d", "rstd_d", "xn_d",
                 "xT_p", "xT_d", "qk_p", "gl_p", "qk_d", "gl_d", "gm_d", "gn_d", "gex_d", "ginv_d", "v_d", "hi_d", "lo_d",
                 "qS_p", "kS_p", "qS_d", "kS_d", "m_p", "red_d", "mall_d", "mhead_d", "mneg_d", "mS_p", "mS_d", "t_p", "exp_d",
                 "out_p", "outT_d", "o2_p", "rden_d", "gate_d", "o_d", "oT_p", "oT_d", "y_p", "xb_d", "x1_d", "stats2_d",
                 "mv2_d", "veps2_d", "rstd2_d", "xn2_d", "x2T_p", "x2T_d", "lg_p", "lg_d", "x1_s", "xn2_s",
                 "xlo_d", "olo_d", "x2lo_d", "x_next")
        (x_first, x_loaded, fill, dfill, consts, stats_d, mv_d, veps_d, rstd_d, xn_d,
         xT_p, xT_d, qk_p, gl_p, qk_d, gl_d, gm_d, gn_d, gex_d, ginv_d, v_d, hi_d, lo_d,
         qS_p, kS_p, qS_d, kS_d, m_p, red_d, mall_d, mhead_d, mneg_d, mS_p, mS_d, t_p, exp_d,
         out_p, outT_d, o2_p, rden_d, gate_d, o_d, oT_p, oT_d, y_p, xb_d, x1_d, stats2_d,
         mv2_d, veps2_d, rstd2_d, xn2_d, x2T_p, x2T_d, lg_p, lg_d, x1_s, xn2_s, xlo_d, olo_d, x2lo_d, x_next) = (sem(n) for n in NAMES)
        X, QK, T1, M0, M1, P0, P1, O = k.bank
        MB, PB = [M0, M1], [P0, P1]
        XCHUNK = 4
        LO, HI, LAST = 5, 29, TILES + 2

        def at_tile(t):
            return k.x[:, bass.ds(t, 1), :].squeeze(1)

        with nc.Block() as block:
            @block.sync
            def _(sp):
                x_view = x_in.rearrange("(t p) d -> p t d", p=P)
                sp.dma_start(k.x[:, 0:1, :], x_view[:, 0:1, :]).then_inc(x_first, 16)
                sp.dma_start(k.x[:, 1:XCHUNK, :], x_view[:, 1:XCHUNK, :]).then_inc(x_next, 16)
                for g in range(1, TILES // XCHUNK):
                    sp.dma_start(k.x[:, g * XCHUNK:(g + 1) * XCHUNK, :],
                                 x_view[:, g * XCHUNK:(g + 1) * XCHUNK, :]).then_inc(x_loaded, 16)

                def slot(i, p):
                    t = i - 2
                    if active(t):
                        sp.wait_ge(x1_d, t + 1)
                        sp.dma_start(x_base[bass.ds(t * P, P), :], x1[:, p % 2, :]).then_inc(x1_s, 16)
                        sp.wait_ge(xn2_d, t + 1)
                        sp.dma_start(rows[bass.ds(t * P, P), 0:D], xn2[:, p % 2, :]).then_inc(xn2_s, 16)
                pipeline(sp, slot, 2, LO, HI, LAST, 4, 4)
                sp.wait_ge(x1_s, 16 * TILES)
                sp.wait_ge(xn2_s, 16 * TILES)

            @block.gpsimd
            def _(pool):
                pool.memset(v1[:, :, :, :], 1.0).then_inc(fill, 1)
                pool.memset(kS[:, :, :, :], 0.0).then_inc(fill, 1)

                def slot(i, p):
                    t, q = i + 2, p % 2
                    if active(t):
                        pool.wait_ge(mv_d, t + 1)
                        pool.tensor_tensor(veps[:, q, 0:1], mv[:, q, 1:2], k.eps[:, :], ALU.add).then_inc(veps_d, 1)
                        pool.wait_ge(veps_d, t + 1)
                        pool.tensor_tensor(rstd[:, q, 0:1], veps[:, q, 0:1], k.half[:, :], ALU.pow).then_inc(rstd_d, 1)
                    t, q = i, p % 2
                    if active(t):
                        pool.wait_ge(xn_d, t + 1)
                        if later(t, 2):
                            pool.wait_ge(x1_d, t - 1)
                        pool.tensor_tensor(xb[:, q, :], at_tile(t), b_p[:, :], ALU.add).then_inc(xb_d, 1)
                    t, q = i - 2, p % 2
                    if active(t):
                        pool.wait_ge(mv2_d, t + 1)
                        pool.tensor_tensor(veps2[:, q, 0:1], mv2[:, q, 1:2], k.eps[:, :], ALU.add).then_inc(veps2_d, 1)
                        pool.wait_ge(veps2_d, t + 1)
                        pool.tensor_tensor(rstd2[:, q, 0:1], veps2[:, q, 0:1], k.half[:, :], ALU.pow).then_inc(rstd2_d, 1)
                pipeline(pool, slot, -2, LO, HI, LAST, 4, 4)

            @block.vector
            def _(dve):
                dve.memset(stack[:, :, :, :, 3, :].rearrange("p q n h d -> p (q n) h d"), 0.0).then_inc(dfill, 1)
                dve.memset(pen[:, :, :], 0.0).then_inc(dfill, 1)
                dve.wait_ge(dfill, 2)
                dve.memset(stack[:, :, 1, :, 3, 0], TOP).then_inc(dfill, 1)
                for b in range(B):
                    dve.memset(pen[:, 0, b * SEQ_TILES:b * SEQ_TILES + 1], -BIG).then_inc(dfill, 1)
                    dve.memset(pen[:, 1, b * SEQ_TILES:b * SEQ_TILES + 2], -BIG).then_inc(dfill, 1)
                dve.wait_ge(dfill, 7)
                dve.memset(gsum[:, :, :], 0.0).then_inc(consts, 1)
                dve.wait_ge(fill, 2)

                def maxima(t, g):
                    dve.wait_ge(m_p, t * 6 + (g + 1))
                    bank = MB[g % 2]
                    if g < 4:
                        dve.reduce_max(mdiag[:, 4 * g:4 * g + 4], bank[:, :].rearrange("p (h s) -> p h s", s=P),
                                       AX.X).then_inc(red_d, 1)
                        return
                    strips = [s for s in TIED[g - 4][0] if s[0] < 8]
                    for h, back, n, at in strips:
                        dst = mtied[:, place_of(h):place_of(h) + 1] if back == 1 else mfar[:, 0:1]
                        dve.reduce_max(dst, bank[:, at:at + n], AX.X)
                    at = [s[3] for s in TIED[g - 4][0] if s[0] >= 8][0]
                    n = REACH[H - 1]
                    first = place_of(8 + g - 4)
                    dve.reduce_max(mtied[:, first:first + 4], bank[:, at:at + 4 * n].rearrange("p (h s) -> p h s", s=n),
                                   AX.X).then_inc(red_d, 1)

                def slot(i, p):
                    t, q = i + 1, (p + 1) % 2
                    if active(t):
                        dve.wait_ge(xT_d, t + 1)
                        dve.tensor_tensor(xT[:, q, 1, :, :], X[:, 0:D].rearrange("p (c t) -> p c t", c=C),
                                          xT[:, q, 0, :, :], ALU.subtract).then_inc(xlo_d, 1)
                    t = i
                    if active(t):
                        if later(t, 1):
                            dve.wait_ge(mneg_d, t)
                        maxima(t, 0)
                        maxima(t, 1)
                    t, q = i - 3, (p + 1) % 2
                    if active(t):
                        dve.wait_ge(rstd2_d, t + 1)
                        dve.wait_ge(mv2_d, t + 1)
                        if later(t, 2):
                            dve.wait_ge(x2T_p, t - 1)
                        if later(t, 1):
                            dve.wait_ge(xn2_s, t * 16)
                        dve.tensor_scalar(xn2[:, q, :], x1[:, q, :], mv2[:, q, 0:1], rstd2[:, q, 0:1],
                                          ALU.subtract, ALU.mult).then_inc(xn2_d, 1)
                    t, q = i - 2, p % 2
                    if active(t):
                        o2 = T1[:, :].rearrange("p (h c) -> p h c", h=H)
                        dve.wait_ge(o2_p, t + 1)
                        dve.reciprocal(rden[:, q, :], o2[:, :, HD]).then_inc(rden_d, 1)
                        dve.wait_ge(rden_d, t + 1)
                        dve.scalar_tensor_tensor(gate[:, q, :], gex[:, (p - 2) % 4, :], ginv[:, (p - 2) % 4, 0:1], rden[:, q, :],
                                                 ALU.mult, ALU.mult).then_inc(gate_d, 1)
                        dve.wait_ge(gate_d, t + 1)
                        dve.tensor_tensor(o[:, q, :, :], o2[:, :, 0:HD],
                                          gate[:, q, :].unsqueeze(2).broadcast_to([P, H, HD]), ALU.mult).then_inc(o_d, 1)
                    t, q = i, p % 2
                    if active(t):
                        dve.tensor_copy(penalty[:, q, :], pen[:, :, bass.ds(t, 1)].squeeze(2))
                        maxima(t, 2)
                    t, q = i + 2, p % 2
                    if active(t):
                        dve.wait_ge(x_first, 16)
                        if later(t, 1):
                            dve.wait_ge(x_next, 16)
                        if later(t, XCHUNK):
                            dve.wait_ge(x_loaded, 16 * (TILES // XCHUNK - 1))
                        dve.bn_stats(stats[:, q, 0:6], at_tile(t)).then_inc(stats_d, 1)
                        dve.wait_ge(stats_d, t + 1)
                    t = i
                    if active(t):
                        maxima(t, 3)
                    t, q = i + 2, p % 2
                    if active(t):
                        dve.bn_aggr(mv[:, q, 0:2], stats[:, q, 0:6]).then_inc(mv_d, 1)
                    t, q, r = i + 1, (p + 1) % 2, (p + 1) % 4
                    if active(t):
                        dve.wait_ge(qk_p, t + 1)
                        dve.scalar_tensor_tensor(qk[:, q, :], QK[:, :], 1 / WS, b_qk[:, :], ALU.mult, ALU.add).then_inc(qk_d, 1)
                        dve.wait_ge(gl_p, t + 1)
                        dve.scalar_tensor_tensor(gl[:, r, :], X[:, 0:H], 1 / WS, b_g[:, :], ALU.mult, ALU.add).then_inc(gl_d, 1)
                    t, q, r = i + 1, (p + 1) % 2, (p + 1) % 4
                    if active(t):
                        dve.wait_ge(qk_d, t + 1)
                        if later(t, 2):
                            dve.wait_ge(kS_p, t - 1)
                            dve.wait_ge(mS_p, t - 1)
                        qv = qk[:, q, :].rearrange("p (n h d) -> p n h d", n=2, h=H)
                        dve.tensor_copy(stack[:, q, 0, :, 0:2, :],
                                        qv[:, 0, :, :].unsqueeze(2).broadcast_to([P, H, 2, HD])).then_inc(hi_d, 1)
                        dve.memset(stack[:, q, 0, :, 3, 0], 0.0).then_inc(hi_d, 1)
                    t, q, r = i + 1, (p + 1) % 2, (p + 1) % 4
                    if active(t):
                        dve.wait_ge(gl_d, t + 1)
                        dve.reduce_max(gm[:, r, 0:1], gl[:, r, :], AX.X).then_inc(gm_d, 1)
                    t, q = i - 2, p % 2
                    if active(t):
                        dve.wait_ge(oT_d, t + 1)
                        dve.tensor_tensor(oT[:, q, 1, :, :], T1[:, 0:D].rearrange("p (c t) -> p c t", c=C),
                                          oT[:, q, 0, :, :], ALU.subtract).then_inc(olo_d, 1)
                    t, q, r = i + 1, (p + 1) % 2, (p + 1) % 4
                    if active(t):
                        dve.wait_ge(gm_d, t + 1)
                        dve.tensor_scalar(gm[:, r, 1:2], gm[:, r, 0:1], -1.0, None, ALU.mult).then_inc(gn_d, 1)
                    t, q, r = i + 1, (p + 1) % 2, (p + 1) % 4
                    if active(t):
                        qv = qk[:, q, :].rearrange("p (n h d) -> p n h d", n=2, h=H)
                        dve.wait_ge(hi_d, (t + 1) * 3)
                        dve.tensor_tensor(stack[:, q, 0, :, 2, :], qv[:, 0, :, :], stack[:, q, 0, :, 0, :],
                                          ALU.subtract).then_inc(lo_d, 1)
                        dve.tensor_tensor(stack[:, q, 1, :, 1, :], qv[:, 1, :, :], stack[:, q, 1, :, 0, :],
                                          ALU.subtract).then_inc(lo_d, 1)
                    t, q = i, p % 2
                    if active(t):
                        maxima(t, 4)
                        maxima(t, 5)
                    t, q = i - 3, (p + 1) % 2
                    if active(t):
                        dve.wait_ge(x2T_d, t + 1)
                        dve.tensor_tensor(x2T[:, q, 1, :, :], X[:, 0:D].rearrange("p (c t) -> p c t", c=C),
                                          x2T[:, q, 0, :, :], ALU.subtract).then_inc(x2lo_d, 1)
                    t, q = i, p % 2
                    if active(t):
                        dve.wait_ge(red_d, (t + 1) * 6)
                        dve.scalar_tensor_tensor(mall[:, q, :], mtied[:, :], pen[:, 0, bass.ds(t, 1)], mdiag[:, :],
                                                 ALU.add, ALU.max).then_inc(mall_d, 1)
                    t, q = i - 2, p % 2
                    if active(t):
                        dve.wait_ge(y_p, t + 1)
                        dve.wait_ge(xb_d, t + 1)
                        if later(t, 1):
                            dve.wait_ge(x1_s, t * 16)
                        dve.scalar_tensor_tensor(x1[:, q, :], T1[:, 0:D], 1 / WS, xb[:, q, :], ALU.mult, ALU.add).then_inc(x1_d, 1)
                    t, q = i, p % 2
                    if active(t):
                        dve.wait_ge(mall_d, t + 1)
                        dve.scalar_tensor_tensor(mall[:, q, 0:1], mfar[:, 0:1], pen[:, 1, bass.ds(t, 1)], mall[:, q, 0:1],
                                                 ALU.add, ALU.max).then_inc(mhead_d, 1)
                    t, q = i - 2, p % 2
                    if active(t):
                        dve.wait_ge(x1_d, t + 1)
                        dve.bn_stats(stats2[:, q, 0:6], x1[:, q, :]).then_inc(stats2_d, 1)
                        dve.wait_ge(stats2_d, t + 1)
                    t, q = i, p % 2
                    if active(t):
                        dve.wait_ge(mhead_d, t + 1)
                        dve.wait_ge(qS_p, t + 1)
                        dve.tensor_scalar(stack[:, q, 0, :, 3, 0].rearrange("p (a j b) -> p a b j", a=2, b=2),
                                          mall[:, q, :].rearrange("p (a b j) -> p a b j", a=2, b=2), -1.0 / TOP, None,
                                          ALU.mult).then_inc(mneg_d, 1)
                    t, r = i + 1, (p + 1) % 4
                    if active(t):
                        dve.wait_ge(kS_p, t + 1)
                        dve.tensor_copy(kS[:, r, :, :], QK[:, :].bitcast(fp16).rearrange("p (h t) -> p h t", t=P)).then_inc(kS_d, 1)
                        dve.wait_ge(gex_d, t + 1)
                        dve.reciprocal(ginv[:, r, 0:1], gsum[:, r, 0:1]).then_inc(ginv_d, 1)
                    t, q = i - 2, p % 2
                    if active(t):
                        dve.bn_aggr(mv2[:, q, 0:2], stats2[:, q, 0:6]).then_inc(mv2_d, 1)
                    t, q = i + 2, p % 2
                    if active(t):
                        dve.wait_ge(rstd_d, t + 1)
                        dve.wait_ge(mv_d, t + 1)
                        if later(t, 2):
                            dve.wait_ge(xT_p, t - 1)
                        dve.tensor_scalar(xn[:, q, :], at_tile(t), mv[:, q, 0:1], rstd[:, q, 0:1],
                                          ALU.subtract, ALU.mult).then_inc(xn_d, 1)
                pipeline(dve, slot, -2, LO, HI, LAST, 4, 4)

            @block.scalar
            def _(act):
                act.wait_ge(consts, 1)
                act.wait_ge(fill, 2)

                def expo(t, par, n, g):
                    act.wait_ge(t_p, t * 6 + (n + 1))
                    if n < 2:
                        width = TIED[n][1]
                        if n == 0:
                            act.activation(pt[:, 0:P], PB[0][:, 0:P], ACT.Exp, bias=penalty[:, par, 1:2], scale=SCALE)
                        at = P if n == 0 else 0
                        act.activation(pt[:, TIED_AT[n] + at:TIED_AT[n] + width], PB[n][:, at:width], ACT.Exp,
                                       bias=penalty[:, par, 0:1], scale=SCALE).then_inc(exp_d, 1)
                    else:
                        act.activation(pd[:, g, :, :], PB[n % 2][:, :].rearrange("p (h t) -> p h t", t=P), ACT.Exp,
                                       scale=SCALE).then_inc(exp_d, 1)

                def slot(i, p):
                    t, q = i + 1, (p + 1) % 2
                    if active(t):
                        act.wait_ge(xT_p, t + 1)
                        if later(t, 2):
                            act.wait_ge(gl_p, t - 1)
                        act.activation(xT[:, q, 0, :, :], X[:, 0:D].rearrange("p (c t) -> p c t", c=C), ACT.Copy).then_inc(xT_d, 1)
                    t = i - 1
                    if active(t):
                        if later(t, 1):
                            act.wait_ge(out_p, t)
                        expo(t, (p + 1) % 2, 0, 0)
                        expo(t, (p + 1) % 2, 1, 0)
                        expo(t, (p + 1) % 2, 2, 0)
                        expo(t, (p + 1) % 2, 3, 1)
                    t, q = i - 2, p % 2
                    if active(t):
                        act.wait_ge(oT_p, t + 1)
                        if later(t, 2):
                            act.wait_ge(y_p, t - 1)
                        act.activation(oT[:, q, 0, :, :], T1[:, 0:D].rearrange("p (c t) -> p c t", c=C), ACT.Copy).then_inc(oT_d, 1)
                    t, q = i + 1, (p + 1) % 2
                    if active(t):
                        act.wait_ge(qk_d, t + 1)
                        if later(t, 2):
                            act.wait_ge(kS_p, t - 1)
                        act.activation(stack[:, q, 1, :, 0:3:2, :],
                                       qk[:, q, D:2 * D].rearrange("p (h d) -> p h d", h=H).unsqueeze(2).broadcast_to([P, H, 2, HD]),
                                       ACT.Copy).then_inc(hi_d, 1)
                    t, r = i + 1, (p + 1) % 4
                    if active(t):
                        act.wait_ge(gn_d, t + 1)
                        act.activation(gex[:, r, :], gl[:, r, :], ACT.Exp, bias=gm[:, r, 1:2],
                                       accum_out=gsum[:, r, 0:1]).then_inc(gex_d, 1)
                    t, q = i - 3, (p + 1) % 2
                    if active(t):
                        act.wait_ge(x2T_p, t + 1)
                        if later(t, 2):
                            act.wait_ge(lg_p, t - 1)
                        act.activation(x2T[:, q, 0, :, :], X[:, 0:D].rearrange("p (c t) -> p c t", c=C), ACT.Copy).then_inc(x2T_d, 1)
                    t = i - 1
                    if active(t):
                        expo(t, (p + 1) % 2, 4, 2)
                        expo(t, (p + 1) % 2, 5, 3)
                    t, q = i + 1, (p + 1) % 2
                    if active(t):
                        act.wait_ge(qS_p, t + 1)
                        act.activation(qS[:, q, :, :], T1[:, :].bitcast(fp16).rearrange("p (h t) -> p h t", t=P), ACT.Copy).then_inc(qS_d, 1)
                    t = i - 3
                    if active(t):
                        act.wait_ge(lg_p, t + 1)
                        act.activation(k.logits[:, bass.ds(t, 1), :].squeeze(1), X[:, 0:E], ACT.Copy, scale=1 / WS).then_inc(lg_d, 1)
                    t, q = i - 1, (p + 1) % 2
                    if active(t):
                        act.wait_ge(out_p, t + 1)
                        if later(t, 2):
                            act.wait_ge(o2_p, t - 1)
                        act.activation(outT[:, q, :, :], O[:, :].rearrange("p (g t) -> p g t", g=4), ACT.Copy).then_inc(outT_d, 1)
                    t, q, r = i + 1, (p + 1) % 2, (p + 1) % 4
                    if active(t):
                        act.wait_ge(qk_d, t + 1)
                        for a in range(2):
                            last = act.activation(
                                v1[:, r, 8 * a:8 * a + 8, 0:HD].rearrange("p (b j) d -> p b j d", b=2),
                                qk[:, q, D + a * P:D + (a + 1) * P].rearrange("p (j b d) -> p b j d", b=2, d=HD), ACT.Copy)
                        last.then_inc(v_d, 1)
                    t, q = i, p % 2
                    if active(t):
                        act.wait_ge(mS_p, t + 1)
                        if later(t, 2):
                            act.wait_ge(t_p, (t - 1) * 6)
                        act.activation(qM[:, q, :, :], T1[:, :].bitcast(fp16).rearrange("p (h t) -> p h t", t=P), ACT.Copy).then_inc(mS_d, 1)
                pipeline(act, slot, -1, LO, HI, LAST, 4, 4)

            @block.tensor
            def _(pe):
                pe.wait_ge(consts, 1)
                pe.wait_ge(fill, 2)

                def transpose2(bank, src, done):
                    for c in range(C):
                        last = pe.transpose(bank[:, c * P:(c + 1) * P], src[:, c * P:(c + 1) * P], k.ident[:, :])
                    last.then_inc(done, 1)

                def q_stack(t, q, done):
                    for h in range(H // 2):
                        last = pe.transpose(T1[:, :].bitcast(fp16)[:, h * P:(h + 1) * P],
                                            stack[:, q, 0, 2 * h:2 * h + 2, :, :].rearrange("p h n d -> p (h n d)"), k.ident16[:, :])
                    last.then_inc(done, 1)

                def for_max(t, p, n):
                    if n >= 2 or later(t, 1):
                        pe.wait_ge(red_d, t * 6 + (n - 1))
                    q, r = p % 2, 64 * (n % 2)
                    bank = MB[n % 2]
                    if n < 4:
                        pe.matmul(bank[:, :], k.identb[:, :], mask_q[:, n, :, :].rearrange("p h s -> p (h s)"), start=True, stop=True,
                                  skip_group_check=True)
                        for j in range(4):
                            h = head(n, j)
                            last = pe.matmul(bank[:, j * P:(j + 1) * P], qS[r:r + 64, q, h // 2, :],
                                             kS[r:r + 64, p % 4, h // 2, :], start=False, stop=True, skip_group_check=True)
                    else:
                        strips, width = TIED[n - 4]
                        pe.matmul(bank[:, 0:width], k.identb[:, :], tied_q[:, TIED_AT[n - 4]:TIED_AT[n - 4] + width],
                                  start=True, stop=True, skip_group_check=True)
                        for h, back, m, at in strips:
                            last = pe.matmul(bank[:, at:at + m], qS[r:r + 64, q, h // 2, :],
                                             kS[r:r + 64, (p - back) % 4, h // 2, P - m:P], start=False, stop=True,
                                             skip_group_check=True)
                    last.then_inc(m_p, 1)

                def for_exp(t, p, n):
                    if n >= 2 or later(t, 1):
                        pe.wait_ge(exp_d, t * 6 + (n - 1))
                    q, r = p % 2, 64 * (n % 2)
                    bank = PB[n % 2]
                    if n < 2:
                        strips, width = TIED[n]
                        pe.matmul(bank[:, 0:width], k.identb[:, :], tied_k[:, TIED_AT[n]:TIED_AT[n] + width],
                                  start=True, stop=True, skip_group_check=True)
                    else:
                        strips = [(head(n - 2, j), 0, P, j * P) for j in range(4)]
                        pe.matmul(bank[:, :], k.identb[:, :], mask_k[:, n - 2, :, :].rearrange("p h s -> p (h s)"), start=True, stop=True,
                                  skip_group_check=True)
                    for h, back, m, at in strips:
                        last = pe.matmul(bank[:, at:at + m], kS[r:r + 64, (p - back) % 4, h // 2, :],
                                         qM[r:r + 64, q, h // 2, 0:m], start=False, stop=True, skip_group_check=True)
                    last.then_inc(t_p, 1)

                def attend(t, p, n):
                    pe.wait_ge(exp_d, t * 6 + (n + 1))
                    if n < 2:
                        todo = [(h, back, m, pt[:, TIED_AT[n] + at:TIED_AT[n] + at + m]) for h, back, m, at in TIED[n][0]]
                    else:
                        todo = [(head(n - 2, j), 0, P, pd[:, n - 2, j, :]) for j in range(4)]
                    for h, back, m, src in todo:
                        g, j = divmod(place_of(h), 4)
                        last = pe.matmul(O[32 * j:32 * j + 32, g * P:g * P + m], v1[:, (p - back) % 4, place_of(h), :], src,
                                         start=(n == 2), stop=True, skip_group_check=True)
                    return last

                def slot(i, p):
                    t, q = i + 1, (p + 1) % 2
                    if active(t):
                        pe.wait_ge(xn_d, t + 1)
                        if later(t, 5):
                            pe.wait_ge(lg_d, t - 4)
                        elif t > 0:
                            pe.wait_ge(gl_d, t)
                        transpose2(X, xn[:, q, :], xT_p)
                    t = i
                    if active(t):
                        pe.wait_ge(qS_d, t + 1)
                        pe.wait_ge(kS_d, t + 1)
                        for_max(t, p, 0)
                        for_max(t, p, 1)
                    t = i - 1
                    if active(t):
                        pe.wait_ge(mS_d, t + 1)
                        for_exp(t, p - 1, 0)
                        for_exp(t, p - 1, 1)
                    t, q = i - 2, p % 2
                    if active(t):
                        pe.wait_ge(outT_d, t + 1)
                        if active(i - 1):
                            pe.wait_ge(mS_d, t + 2)
                        else:
                            pe.wait_ge(x1_d, t)
                        for g in range(4):
                            last = pe.transpose(T1[:, g * P:(g + 1) * P], outT[:, q, g, :], k.ident[:, :])
                        last.then_inc(o2_p, 1)
                    t, q = i + 1, (p + 1) % 2
                    if active(t):
                        pe.wait_ge(xlo_d, t + 1)
                        if later(t, 1):
                            pe.wait_ge(kS_d, t)
                        split_product(pe, QK[:, :], xT[:, q, :, :, :], w16[:, :, :, :]).then_inc(qk_p, 1)
                        split_product(pe, X[:, 0:H], xT[:, q, :, :, :], w_g16[:, :, :, :]).then_inc(gl_p, 1)
                    t = i
                    if active(t):
                        for_max(t, p, 2)
                        for_max(t, p, 3)
                    t = i - 1
                    if active(t):
                        for_exp(t, p - 1, 2)
                        for_exp(t, p - 1, 3)
                    t, q = i - 2, p % 2
                    if active(t):
                        pe.wait_ge(o_d, t + 1)
                        transpose2(T1, o[:, q, :, :].rearrange("p h d -> p (h d)"), oT_p)
                    t = i
                    if active(t):
                        for_max(t, p, 4)
                        for_max(t, p, 5)
                    t = i - 1
                    if active(t):
                        pe.wait_ge(v_d, t + 1)
                        if later(t, 1):
                            pe.wait_ge(outT_d, t)
                        attend(t, p - 1, 2)
                        attend(t, p - 1, 3)
                    t, q = i - 3, (p + 1) % 2
                    if active(t):
                        pe.wait_ge(xn2_d, t + 1)
                        if active(i + 1):
                            pe.wait_ge(gl_d, t + 5)
                        else:
                            pe.wait_ge(lg_d, t)
                        transpose2(X, xn2[:, q, :], x2T_p)
                    t, q = i - 2, p % 2
                    if active(t):
                        pe.wait_ge(olo_d, t + 1)
                        split_product(pe, T1[:, 0:D], oT[:, q, :, :, :], w_p16[:, :, :, :]).then_inc(y_p, 1)
                    t = i - 1
                    if active(t):
                        for_exp(t, p - 1, 4)
                        for_exp(t, p - 1, 5)
                    t = i - 1
                    if active(t):
                        attend(t, p - 1, 0)
                        attend(t, p - 1, 1)
                    t, q = i + 1, (p + 1) % 2
                    if active(t):
                        pe.wait_ge(lo_d, (t + 1) * 2)
                        if later(t, 3):
                            pe.wait_ge(x1_d, t - 2)
                        elif t == 2:
                            pe.wait_ge(mS_d, 1)
                        elif t == 1:
                            pe.wait_ge(qS_d, 1)
                        q_stack(t, q, qS_p)
                        for h in range(H // 2):
                            last = pe.transpose(QK[:, :].bitcast(fp16)[:, h * P:(h + 1) * P],
                                                stack[:, q, 1, 2 * h:2 * h + 2, :, :].rearrange("p h n d -> p (h n d)"), k.ident16[:, :])
                        last.then_inc(kS_p, 1)
                    t, q = i - 3, (p + 1) % 2
                    if active(t):
                        pe.wait_ge(x2lo_d, t + 1)
                        split_product(pe, X[:, 0:E], x2T[:, q, :, :, :], k.wg16[:, :, :, :], all_terms=True).then_inc(lg_p, 1)
                    t = i - 1
                    if active(t):
                        attend(t, p - 1, 4)
                        attend(t, p - 1, 5).then_inc(out_p, 1)
                    t, q = i, p % 2
                    if active(t):
                        pe.wait_ge(mneg_d, t + 1)
                        if active(i + 1):
                            pe.wait_ge(qS_d, t + 2)
                        else:
                            pe.wait_ge(x1_d, t - 1)
                        q_stack(t, q, mS_p)
                pipeline(pe, slot, -1, LO, HI, LAST, 4, 4)



def hybrid_block(nc, x, wq, wk, wv, wo, wqk, bqk, w_gate, b_gate, w_proj, b_proj, gate_wt, w1t, w2t, out):
    def scratch(name, shape, dt):
        return nc.dram_tensor(name, shape, dt, kind="Internal").ap()

    middle = scratch("middle", [N, D], fp32)
    with ExitStack() as ctx:
        k = Core(nc, ctx)
        rows = scratch("rows_a", [N, ROW], fp32)
        with nc.cleanup_on_exit():
            setup(nc, k, gate_wt)
            linear_attention(nc, k, x, wq, wk, wv, wo, middle, rows)
        with nc.cleanup_on_exit():
            router(nc, k, "ra", rows, window=(wqk, bqk, w_gate, b_gate, w_proj, b_proj))
            experts(nc, k, "fa", rows, w1t, w2t, middle)
        rows = scratch("rows_b", [N, ROW], fp32)
        with nc.cleanup_on_exit():
            windowed_attention(nc, k, middle, out, rows)
        with nc.cleanup_on_exit():
            router(nc, k, "rb", rows)
            experts(nc, k, "fb", rows, w1t, w2t, out)


def kernel(**inputs):
    import numpy as np
    import concourse.bacc as bacc
    from concourse.bass_utils import run_bass_kernel_spmd

    a = {n: np.asarray(v) for n, v in inputs.items()}

    def by_place(w):
        return w.reshape(2, 4, 2, HD, -1).transpose(0, 2, 1, 3, 4).reshape(w.shape)

    places = np.arange(H).reshape(2, 4, 2).transpose(0, 2, 1).reshape(-1)
    b = {
        "x": a["L0_attn_a_x"].reshape(N, D),
        "wq": a["L0_attn_a_wq"],
        "wk": a["L0_attn_a_wk"],
        "wv": by_place(a["L0_attn_a_wv"].T).T,
        "wo": by_place(a["L0_attn_a_wo"]),
        "wqk": a["L0_attn_b_Wqk"],
        "bqk": a["L0_attn_b_bqk"],
        "w_gate": a["L0_attn_b_Wgate"][:, places],
        "b_gate": a["L0_attn_b_bgate"][places],
        "w_proj": by_place(a["L0_attn_b_Wproj"]),
        "b_proj": a["L0_attn_b_bproj"],
        "gate_wt": a["L0_ffn_gate_w"].T,
        "w1t": a["L0_ffn_w1"].transpose(0, 2, 1).reshape(E * D, F),
        "w2t": a["L0_ffn_w2"].transpose(0, 2, 1).reshape(E * F, D),
    }
    nc = bacc.Bacc("TRN2", target_bir_lowering=False, num_devices=1)
    arrays, args = {}, []
    for name, value in b.items():
        value = np.ascontiguousarray(value)
        arrays[f"in_{name}_dram"] = value
        args.append(nc.dram_tensor(f"in_{name}_dram", value.shape, mybir.dt.from_np(value.dtype), kind="ExternalInput").ap())
    args.append(nc.dram_tensor("out_dram", [N, D], fp32, kind="ExternalOutput").ap())
    hybrid_block(nc, *args)
    r = run_bass_kernel_spmd(nc, [arrays], core_ids=[0])
    return np.asarray(r.results[0]["out_dram"]).reshape(B, S, D)
```
